# Optimizing a Trainium2 kernel written in Bass

```python
import numpy as np
import jax
import jax.numpy as jnp

def _softmax(x, axis=-1):
    return jax.nn.softmax(x, axis=axis)

def _gelu(x):
    return jax.nn.gelu(x, approximate=True)

def _silu(x):
    return jax.nn.silu(x)

def _sigmoid(x):
    return jax.nn.sigmoid(x)

def _layernorm(x, axis=-1, eps=1e-05):
    m = jnp.mean(x, axis=axis, keepdims=True)
    v = jnp.var(x, axis=axis, keepdims=True)
    return (x - m) / jnp.sqrt(v + eps)

def _scatter_add(tgt, idx, src, axis=0):
    return tgt.at[idx].add(src)

def _segment_sum(src, seg, n):
    return jax.ops.segment_sum(src, seg, n)
kernel_name = 'mk_gnn_preln_d2_gnn_r8_231b46'

def setup_inputs(seed: int=0):
    np.random.seed(seed)
    _w = jnp.asarray

    def _rec_inputs():
        import jax
        import jax.numpy as jnp
        _gk = jax.random.key(seed)
        x = -0.000202 + 1 * jax.random.normal(jax.random.fold_in(_gk, 1), (12500, 128), jnp.float32)
        _s = jax.random.randint(jax.random.fold_in(_gk, 2), (200000,), 0, 12500, jnp.int32)
        _d = jax.random.randint(jax.random.fold_in(_gk, 3), (200000,), 0, 12500, jnp.int32)
        _loop = jnp.arange(12500, dtype=jnp.int32)
        src = jnp.concatenate([_s, _d, _loop])
        dst = jnp.concatenate([_d, _s, _loop])
        _o = jnp.argsort(dst, stable=True)
        src = src[_o]
        dst = dst[_o]
        edge_attr_16 = 0.000254156 + 0.999948 * jax.random.normal(jax.random.fold_in(_gk, 11), (412500, 16), jnp.float32)
        edge_weight = jax.random.uniform(jax.random.fold_in(_gk, 13), (412500,), jnp.float32, 0.0, 0.999998)
        return (x, src, dst, edge_attr_16, edge_weight)
    x, src, dst, edge_attr_16, edge_weight = _rec_inputs()

    def _L0_gnn_setup():
        import jax, jax.numpy as jnp
        import numpy as np
        N = 6250
        E = 100000
        D = 128
        DE = 16
        key = jax.random.key(seed)
        ks = jax.random.split(key, 12)

        def lin(k, fan_in, fan_out):
            bound = 1.0 / np.sqrt(fan_in)
            kw, kb = jax.random.split(k)
            W = jax.random.uniform(kw, (fan_in, fan_out), jnp.float32, -bound, bound)
            b = jax.random.uniform(kb, (fan_out,), jnp.float32, -bound, bound)
            return (W, b)
        x = jax.random.normal(ks[0], (N, D), jnp.float32)
        edge_index = jax.random.randint(ks[1], (2, E), 0, N, jnp.int64)
        edge_attr = jax.random.normal(ks[2], (E, DE), jnp.float32)
        eW1, eb1 = lin(ks[3], 2 * D + DE, D)
        eW2, eb2 = lin(ks[4], D, D)
        nW1, nb1 = lin(ks[5], 2 * D, D)
        nW2, nb2 = lin(ks[6], D, D)
        return {'x': x, 'edge_index': edge_index, 'edge_attr': edge_attr, 'eW1': eW1, 'eb1': eb1, 'eW2': eW2, 'eb2': eb2, 'nW1': nW1, 'nb1': nb1, 'nW2': nW2, 'nb2': nb2}
    _L0_gnn_all = _L0_gnn_setup()
    _L0_gnn_in = {k: v for k, v in _L0_gnn_all.items() if k in ('eW1', 'eb1', 'eW2', 'eb2', 'nW1', 'nb1', 'nW2', 'nb2')}
    del _L0_gnn_all

    def _L1_gnn_setup():
        import jax, jax.numpy as jnp
        import numpy as np
        N = 12500
        E = 125000
        F_IN = 128
        F_OUT = 64
        NHOP = 2

        def _xavier(k, shape, gain=1.414):
            fan_in, fan_out = shape
            std = gain * np.sqrt(2.0 / (fan_in + fan_out))
            return (jax.random.normal(k, shape) * std).astype(jnp.float32)

        def _spmm(row, col, val, v, n):
            return jax.ops.segment_sum(val[:, None] * v[col], row, num_segments=n)

        def _adaptive_enc(y, fc, bf):
            g = jax.nn.sigmoid(y @ fc + bf)
            return jnp.where(y < 0, 0.0, y) + g * jnp.where(y > 0, 0.0, y)
        key = jax.random.key(seed)
        ks = jax.random.split(key, 8)
        x = jax.random.normal(ks[0], (N, F_IN), jnp.float32)
        edge_index = jax.random.randint(ks[1], (2, E), 0, N)
        edge_attr = jax.random.uniform(ks[2], (E,), jnp.float32)
        W0 = _xavier(ks[3], (F_IN, F_OUT))
        W1 = _xavier(ks[4], (F_IN, F_OUT))
        b0 = jnp.zeros((F_OUT,), jnp.float32)
        b1 = jnp.zeros((F_OUT,), jnp.float32)
        fc0 = _xavier(ks[5], (F_OUT, 1))
        fc1 = _xavier(ks[6], (F_OUT, 1))
        bf0 = jnp.zeros((1,), jnp.float32)
        bf1 = jnp.zeros((1,), jnp.float32)
        return dict(x=x, edge_index=edge_index, edge_attr=edge_attr, W0=W0, b0=b0, W1=W1, b1=b1, fc0=fc0, bf0=bf0, fc1=fc1, bf1=bf1)
    _L1_gnn_all = _L1_gnn_setup()
    _L1_gnn_in = {k: v for k, v in _L1_gnn_all.items() if k in ('W0', 'b0', 'W1', 'b1', 'fc0', 'bf0', 'fc1', 'bf1')}
    del _L1_gnn_all
    return {'x': x, 'src': src, 'dst': dst, 'edge_attr_16': edge_attr_16, 'edge_weight': edge_weight, 'L0_gnn_eW1': _L0_gnn_in['eW1'], 'L0_gnn_eb1': _L0_gnn_in['eb1'], 'L0_gnn_eW2': _L0_gnn_in['eW2'], 'L0_gnn_eb2': _L0_gnn_in['eb2'], 'L0_gnn_nW1': _L0_gnn_in['nW1'], 'L0_gnn_nb1': _L0_gnn_in['nb1'], 'L0_gnn_nW2': _L0_gnn_in['nW2'], 'L0_gnn_nb2': _L0_gnn_in['nb2'], 'L1_gnn_W0': _L1_gnn_in['W0'], 'L1_gnn_b0': _L1_gnn_in['b0'], 'L1_gnn_W1': _L1_gnn_in['W1'], 'L1_gnn_b1': _L1_gnn_in['b1'], 'L1_gnn_fc0': _L1_gnn_in['fc0'], 'L1_gnn_bf0': _L1_gnn_in['bf0'], 'L1_gnn_fc1': _L1_gnn_in['fc1'], 'L1_gnn_bf1': _L1_gnn_in['bf1']}

def reference(x, src, dst, edge_attr_16, edge_weight, L0_gnn_eW1, L0_gnn_eb1, L0_gnn_eW2, L0_gnn_eb2, L0_gnn_nW1, L0_gnn_nb1, L0_gnn_nW2, L0_gnn_nb2, L1_gnn_W0, L1_gnn_b0, L1_gnn_W1, L1_gnn_b1, L1_gnn_fc0, L1_gnn_bf0, L1_gnn_fc1, L1_gnn_bf1):
    import jax
    import jax.numpy as jnp

    def _L0_gnn_ref(x, edge_index, edge_attr, eW1, eb1, eW2, eb2, nW1, nb1, nW2, nb2):
        import jax, jax.numpy as jnp
        import numpy as np
        N = 6250
        E = 100000
        D = 128
        DE = 16
        row, col = (edge_index[0], edge_index[1])
        edge_input = jnp.concatenate([x[row], x[col], edge_attr], axis=-1)
        h = jax.nn.silu(edge_input @ eW1 + eb1)
        m_ij = jax.nn.silu(h @ eW2 + eb2)
        agg = jax.ops.segment_sum(m_ij, row, num_segments=x.shape[0])
        node_input = jnp.concatenate([x, agg], axis=-1)
        update = jax.nn.silu(node_input @ nW1 + nb1) @ nW2 + nb2
        return x + update

    def _L1_gnn_ref(x, edge_index, edge_attr, W0, b0, W1, b1, fc0, bf0, fc1, bf1):
        import jax, jax.numpy as jnp
        import numpy as np
        N = 12500
        E = 125000
        F_IN = 128
        F_OUT = 64
        NHOP = 2

        def _xavier(k, shape, gain=1.414):
            fan_in, fan_out = shape
            std = gain * np.sqrt(2.0 / (fan_in + fan_out))
            return (jax.random.normal(k, shape) * std).astype(jnp.float32)

        def _spmm(row, col, val, v, n):
            return jax.ops.segment_sum(val[:, None] * v[col], row, num_segments=n)

        def _adaptive_enc(y, fc, bf):
            g = jax.nn.sigmoid(y @ fc + bf)
            return jnp.where(y < 0, 0.0, y) + g * jnp.where(y > 0, 0.0, y)
        n = x.shape[0]
        row, col = (edge_index[0], edge_index[1])
        ones = jnp.ones((n, 1), x.dtype)
        params = [(W0, b0, fc0, bf0), (W1, b1, fc1, bf1)]
        outs = []
        for hop in range(NHOP):
            W, b, fc, bf = params[hop]
            h = x @ W
            agg, deg = (h, ones)
            for _ in range(hop + 1):
                agg = _spmm(row, col, edge_attr, agg, n)
                deg = _spmm(row, col, edge_attr, deg, n)
            safe_deg = jnp.where(deg > 0, deg, 1.0)
            y = jnp.where(deg > 0, agg / safe_deg, 0.0)
            y = y + b
            outs.append(_adaptive_enc(y, fc, bf))
        return jnp.concatenate(outs, axis=1)
    edge_index = jnp.stack([src, dst])
    h = jnp.maximum(_layernorm(x, axis=-1), 0.0)
    x = x + _L0_gnn_ref(h, edge_index, edge_attr_16, L0_gnn_eW1, L0_gnn_eb1, L0_gnn_eW2, L0_gnn_eb2, L0_gnn_nW1, L0_gnn_nb1, L0_gnn_nW2, L0_gnn_nb2)
    h = jnp.maximum(_layernorm(x, axis=-1), 0.0)
    x = x + _L1_gnn_ref(h, edge_index, edge_weight, L1_gnn_W0, L1_gnn_b0, L1_gnn_W1, L1_gnn_b1, L1_gnn_fc0, L1_gnn_bf0, L1_gnn_fc1, L1_gnn_bf1)
    return x

_drawn_inputs = setup_inputs


def setup_inputs(seed=0):
    import zlib

    import numpy as np

    out = dict(_drawn_inputs(seed))
    spreads = {'L1_gnn_b0': (0.0, 0.1), 'L1_gnn_b1': (0.0, 0.1)}
    factors = {'edge_attr_16': 5.914, 'L0_gnn_eb1': 3.273, 'L0_gnn_nb1': 7.265}
    for name, (base, spread) in spreads.items():
        noise = np.random.default_rng([zlib.crc32(name.encode()), seed]).standard_normal(out[name].shape)
        drawn = base * np.exp(spread * noise) if base else spread * noise
        out[name] = jnp.asarray(drawn.astype(out[name].dtype))
    for name, factor in factors.items():
        out[name] = (out[name] * factor).astype(out[name].dtype)
    return out
```

```python
from contextlib import ExitStack

import concourse.bass as bass
from concourse import mybir

P = 128
D = 128
DE = 16
FO = 64
WORDS = 32
W_AT, LO_AT, DST_AT = 16, 17, 18
GROUP = 2
CH = 4
RING = 4
COLS = 16
EPS = 1e-5
BIG = 53248


def up(a, b):
    return (a + b - 1) // b * b


def wait(eng, s, value):
    if not isinstance(value, int) or value > 0:
        eng.wait_ge(s, value)


def looped(eng, steps, body):
    body(0)
    with eng.Fori(1, steps) as i:
        body(i)


def sizes(n_nodes, n_edges):
    blocks = up(n_nodes + 1, 8 * P) // P
    cols = up(up(n_edges, P) // P, 2 * COLS)
    slots = up(P * cols + blocks * (GROUP * P - 1), RING * CH * P)
    return blocks, cols, slots


def gnn(nc, x, src, edges, w_node, b_node, w_edge, e_w2, e_b2, w_update, n_b2, b_hop, fc, bf, out):
    f32, bf16, i32 = mybir.dt.float32, mybir.dt.bfloat16, mybir.dt.int32
    ALU, ACT, AX = mybir.AluOpType, mybir.ActivationFunctionType, mybir.AxisListType
    NB = x.shape[0] // P
    C = src.shape[1]
    SLOTS = up(P * C + NB * (GROUP * P - 1), RING * CH * P)
    GROUPS = SLOTS // (GROUP * P)
    GC = up(GROUPS, P) // P
    CHUNKS = SLOTS // (CH * P)
    NQ = NB // 4
    HW = 4 * NB
    assert HW <= 512 and NB % 8 == 0 and C % (2 * COLS) == 0 and CHUNKS % RING == 0

    recs = nc.dram_tensor("recs", [SLOTS, WORDS], f32).ap()
    dst_tab = nc.dram_tensor("dst_tab", [NB * P, D], f32).ap()
    node_dr = nc.dram_tensor("node_dr", [NB * P, 2 * D], f32).ap()
    blk_dr = nc.dram_tensor("blk_dr", [GC * P], i32).ap()
    hop_tab = nc.dram_tensor("hop_tab", [NB * P, 2 * FO], f32).ap()
    x1_dr = nc.dram_tensor("x1_dr", [NB * P, D], f32).ap()
    hop2_tab = nc.dram_tensor("hop2_tab", [NB * P, FO + 1], f32).ap()

    ctx = ExitStack()
    with ctx:
        def sb(name, shape, dt=f32, stack=ctx):
            return stack.enter_context(nc.sbuf_tensor(name, shape, dt))

        def sem(name):
            return ctx.enter_context(nc.semaphore(name))

        big_a = sb("big_a", [P, NB, 3 * D // 2])
        big_b = sb("big_b", [P, NB, D])
        src_tab = big_a[:, :, :].bitcast(bf16).rearrange("p b (s f) -> p b s f", s=3)
        ident = sb("ident", [P, P])
        iota_n = sb("iota_n", [P, P])
        eps = sb("eps", [P, 1])
        blk_row = sb("blk_row", [1, GC * P], i32)

        with ExitStack() as st:
            wn = sb("wn", [P, 3 * D], stack=st)
            bn = sb("bn", [P, 3 * D], stack=st)
            h = sb("h", [P, 2, 4, D], stack=st)
            hT = sb("hT", [P, 2, 4, P], stack=st)
            stage = sb("stage", [P, 2, 4, 3 * D], stack=st)
            stats = sb("stats", [P, 2, 4, 6], stack=st)
            mv = sb("mv", [P, 2, 4, 2], stack=st)
            sd = sb("sd", [P, 2, 4], stack=st)
            rstd = sb("rstd", [P, 2, 4], stack=st)
            nmr = sb("nmr", [P, 2, 4], stack=st)
            tmp = sb("tmp", [P, 4, D], stack=st)
            s_sp, s_sd, s_eps, s_turn_v = sem("n_split"), sem("n_std"), sem("n_eps"), sem("n_turn_v")
            ps = st.enter_context(nc.psum_tensor("ps0", [P, 8, 512], f32))
            s_w, s_x, s_id = sem("n_weights"), sem("n_x"), sem("n_consts")
            s_st, s_mv, s_rs, s_nm = sem("n_stats"), sem("n_mean_var"), sem("n_rstd"), sem("n_shift")
            s_h, s_tp, s_hT, s_mm = sem("n_h"), sem("n_hT_psum"), sem("n_hT"), sem("n_products")
            s_ev, s_out = sem("n_evacuated"), [sem("n_stored0"), sem("n_stored1")]
            xq = x.rearrange("(b p) f -> p b f", p=P)
            tab_v = dst_tab.rearrange("(b p) f -> p b f", p=P)
            nod_v = node_dr.rearrange("(b p) f -> p b f", p=P)
            block = st.enter_context(nc.Block())

            @block.sync
            def _(sp):
                sp.dma_start(wn[:, :], w_node).then_inc(s_w, 16)
                sp.dma_start(bn[:, :], b_node.partition_broadcast(P)).then_inc(s_w, 16)
                sp.dma_start(big_b[:, :, :], xq).then_inc(s_x, 16)

                def store(i):
                    for u in range(2):
                        sp.wait_ge(s_ev, i * 6 + 3 * u + 3)
                        sp.dma_start(tab_v[:, bass.ds(i * 8 + 4 * u, 4), :], stage[:, u, :, 0:D]).then_inc(s_out[u], 16)
                        sp.dma_start(nod_v[:, bass.ds(i * 8 + 4 * u, 4), :], stage[:, u, :, D:3 * D]).then_inc(s_out[u], 16)
                looped(sp, NQ // 2, store)
                for u in range(2):
                    sp.wait_ge(s_out[u], NQ // 2 * 32)

            @block.gpsimd
            def _(pool):
                pool.memset(ident[:, :], 0.0).then_inc(s_id, 1)
                pool.wait_ge(s_id, 1)
                pool.affine_select(out=ident[:, :], in_=ident[:, :], compare_op=ALU.not_equal, fill=1.0,
                                   base=0, pattern=[[-1, P]], channel_multiplier=1).then_inc(s_id, 1)
                pool.iota(iota_n[:, :], [[1, P]], 0, 0, allow_small_or_imprecise_dtypes=True).then_inc(s_id, 1)

            @block.vector
            def _(v):
                v.memset(eps[:, :], EPS).then_inc(s_eps, 1)
                v.wait_ge(s_x, 16)
                v.wait_ge(s_w, 32)

                def quads(i):
                    for u in range(2):
                        n = i * 2 + u
                        for t in range(4):
                            v.bn_stats(stats[:, u, t, :], big_b[:, bass.ds(n * 4 + t, 1), :].rearrange("p a f -> p (a f)")).then_inc(s_st, 1)
                        v.wait_ge(s_st, n * 4 + 4)
                        v.sem_inc(s_turn_v, 1)
                        for t in range(4):
                            v.bn_aggr(mv[:, u, t, :], stats[:, u, t, :]).then_inc(s_mv, 1)
                        v.wait_ge(s_mv, n * 4 + 4)
                        v.wait_ge(s_sd, n + 1)
                        v.reciprocal(rstd[:, u, :], sd[:, u, :]).then_inc(s_rs, 1)
                        v.wait_ge(s_rs, n + 1)
                        v.scalar_tensor_tensor(out=nmr[:, u, :], in0=mv[:, u, :, 0], scalar=-1.0, in1=rstd[:, u, :],
                                               op0=ALU.mult, op1=ALU.mult).then_inc(s_nm, 1)
                        wait(v, s_out[u], i * 32)
                        v.wait_ge(s_h, n * 4 + 4)
                        v.tensor_tensor(stage[:, u, :, 2 * D:3 * D], big_b[:, bass.ds(n * 4, 4), :], h[:, u, :, :],
                                        ALU.add).then_inc(s_ev, 1)
                        v.wait_ge(s_mm, n + 1)
                        v.tensor_tensor(tmp[:, :, :], ps[:, 2:6, 0:D],
                                        bn[:, 0:D].unsqueeze(1).to_broadcast([P, 4, D]), ALU.add).then_inc(s_ev, 1)
                        v.wait_ge(s_ev, n * 3 + 2)
                        parts = [src_tab[:, bass.ds(n * 4, 4), s, :] for s in range(3)]
                        for s in range(3):
                            v.tensor_copy(parts[s], tmp[:, :, :]).then_inc(s_sp, 1)
                            v.wait_ge(s_sp, n * 5 + 2 * s + 1)
                            if s < 2:
                                v.tensor_tensor(tmp[:, :, :], tmp[:, :, :], parts[s], ALU.subtract).then_inc(s_sp, 1)
                                v.wait_ge(s_sp, n * 5 + 2 * s + 2)
                        v.tensor_tensor(stage[:, u, :, 0:2 * D], ps[:, 2:6, D:3 * D],
                                        bn[:, D:3 * D].unsqueeze(1).to_broadcast([P, 4, 2 * D]), ALU.add).then_inc(s_ev, 1)
                looped(v, NQ // 2, quads)

            @block.scalar
            def _(act):
                act.wait_ge(s_eps, 1)

                def quads(i):
                    for u in range(2):
                        n = i * 2 + u
                        act.wait_ge(s_mv, n * 4 + 4)
                        act.activation(sd[:, u, :], mv[:, u, :, 1], ACT.Sqrt, bias=eps[:, :]).then_inc(s_sd, 1)
                        act.wait_ge(s_nm, n + 1)
                        for t in range(4):
                            act.activation(h[:, u, t, :], big_b[:, bass.ds(n * 4 + t, 1), :].rearrange("p a f -> p (a f)"), ACT.Relu,
                                           bias=nmr[:, u, t:t + 1], scale=rstd[:, u, t:t + 1]).then_inc(s_h, 1)
                        act.wait_ge(s_tp, n + 1)
                        act.activation(hT[:, u, :, :], ps[:, u, :].rearrange("p (a b) -> p a b", a=4), ACT.Copy).then_inc(s_hT, 1)
                looped(act, NQ // 2, quads)

            @block.tensor
            def _(pe):
                pe.wait_ge(s_id, 3)
                pe.wait_ge(s_w, 32)

                def quads(i):
                    for u in range(2):
                        n = i * 2 + u
                        pe.wait_ge(s_h, n * 4 + 4)
                        for t in range(4):
                            last = pe.transpose(ps[:, u, t * P:(t + 1) * P], h[:, u, t, :], ident[:, :])
                        last.then_inc(s_tp, 1)
                        pe.wait_ge(s_hT, n + 1)
                        wait(pe, s_ev, n * 3)
                        for t in range(4):
                            last = pe.matmul(ps[:, 2 + t, 0:3 * D], hT[:, u, t, :], wn[:, :], start=True, stop=True)
                        last.then_inc(s_mm, 1)
                looped(pe, NQ // 2, quads)

        with ExitStack() as st:
            src_i = sb("src_i", [P, C], i32, stack=st)
            part_i = sb("part_i", [P, C], i32, stack=st)
            lo = part_i[:, :].bitcast(f32)
            hi = sb("hi", [P, C], bf16, stack=st)
            iota_b = sb("iota_b", [P, NB], bf16, stack=st)
            ones = sb("ones", [P, P], bf16, stack=st)
            below = sb("below", [P, P], bf16, stack=st)
            rest = sb("rest", [P, P], bf16, stack=st)
            zero = sb("zero", [P, HW], bf16, stack=st)
            hot = sb("hot", [P, 2, COLS, NB], bf16, stack=st)
            prod = sb("prod", [P, COLS, NB], stack=st)
            pos_f = sb("pos_f", [P, 2, COLS], stack=st)
            pos = sb("pos", [P, 2, COLS], i32, stack=st)
            rec = sb("rec", [P, 2, COLS, WORDS], stack=st)
            fill = sb("fill", [P, 8, WORDS], stack=st)
            tot = prod
            base = sb("base", [P, COLS, NB], stack=st)
            cnt = sb("cnt", [P, 4, NB], stack=st)
            cnt_i = sb("cnt_i", [P, NB], i32, stack=st)
            gval = sb("gval", [P, GC], stack=st)
            cmp = sb("cmp", [P, GC, NB], stack=st)
            blk_f = sb("blk_f", [P, GC], stack=st)
            blk_i = sb("blk_i", [P, GC], i32, stack=st)
            ps = st.enter_context(nc.psum_tensor("ps1", [P, 8, 512], f32))
            s_src, s_fill, s_c, s_chain = sem("s_src"), sem("s_filled"), sem("s_consts"), sem("s_chain")
            s_fz, s_seed = sem('s_fill_ready'), sem('s_seed')
            s_hot, s_used, s_rank, s_prod = sem("s_hot"), sem("s_hot_counted"), sem("s_ranked"), sem("s_prod")
            s_pos, s_base, s_tot = sem("s_pos"), sem("s_base"), sem("s_total")
            s_rec = [sem("s_rec0"), sem("s_rec1")]
            s_lo = sem("s_lo")
            s_sc = [sem("s_scattered0"), sem("s_scattered1")]
            s_blk, s_turn, s_z, s_hot2, s_used2 = sem("s_blk"), sem("s_turn"), sem("s_z"), sem("s_hot2"), sem("s_used2")
            s_red = sem("s_reduced")
            STEPS = C // COLS
            e_v = edges.rearrange("(p c) w -> p c w", p=P)
            FR = 8
            fill_v = recs.rearrange("(n p a) w -> n p (a w)", p=P, a=8)
            NF = fill_v.shape[0]
            block = st.enter_context(nc.Block())

            @block.sync
            def _(sp):
                sp.dma_start(src_i[:, :], src).then_inc(s_src, 16)
                sp.wait_ge(s_fz, 1)
                with sp.Fori(0, NF) as i:
                    sp.dma_start(fill_v[bass.ds(i, 1), :, :].rearrange("a p w -> (a p) w"),
                                 fill[:, :, :].rearrange("p a w -> p (a w)")).then_inc(s_fill, 16)
                for u in range(2):
                    sp.dma_start(rec[:, u, :, :], e_v[:, u * COLS:(u + 1) * COLS, :]).then_inc(s_rec[u], 16)
                with sp.Fori(1, STEPS // 2) as i:
                    for u in range(2):
                        sp.wait_ge(s_sc[u], i * (16 * COLS))
                        sp.dma_start(rec[:, u, :, :], e_v[:, bass.ds((i * 2 + u) * COLS, COLS), :]).then_inc(s_rec[u], 16)
                sp.wait_ge(s_blk, 1)
                sp.dma_start(blk_dr.rearrange("(p c) -> p c", p=P), blk_i[:, :]).then_inc(s_src, 16)
                sp.wait_ge(s_src, 32)
                sp.dma_start(blk_row[:, :], blk_dr.unsqueeze(0)).then_inc(s_src, 16)
                sp.wait_ge(s_src, 48)
                for u in range(2):
                    sp.wait_ge(s_sc[u], STEPS // 2 * 16 * COLS)

            @block.gpsimd
            def _(pool):
                pool.memset(fill[:, :, :], 0.0).then_inc(s_z, 1)
                pool.wait_ge(s_z, 1)
                pool.memset(fill[:, :, LO_AT:LO_AT + 1], -1.0).then_inc(s_fz, 1)
                pool.memset(ones[:, :], 1.0).then_inc(s_z, 1)
                pool.wait_ge(s_z, 2)
                pool.affine_select(out=below[:, :], in_=ones[:, :], compare_op=ALU.is_gt, fill=0.0,
                                   base=0, pattern=[[1, P]], channel_multiplier=-1).then_inc(s_c, 1)
                pool.affine_select(out=rest[:, :], in_=ones[:, :], compare_op=ALU.is_ge, fill=0.0,
                                   base=0, pattern=[[-1, P]], channel_multiplier=1).then_inc(s_c, 1)
                pool.iota(iota_b[:, :], [[1, NB]], 0, 0, allow_small_or_imprecise_dtypes=True).then_inc(s_c, 1)
                pool.iota(gval[:, :], [[GROUP * P, GC]], 0, GROUP * P * GC, allow_small_or_imprecise_dtypes=True).then_inc(s_c, 1)
                pool.wait_ge(s_fill, NF * 16)
                with pool.Fori(0, STEPS // 2) as i:
                    for u in range(2):
                        pool.wait_ge(s_pos, i * 2 + u + 1)
                        pool.sem_inc(s_turn, 1)
                        pool.wait_ge(s_lo, i * 2 + u + 1)
                        pool.sem_inc(s_turn, 1)
                        for j in range(COLS):
                            pool.indirect_dma_start(recs, bass.IndirectOffsetOnAxis(ap=pos[:, u, j:j + 1], axis=0),
                                                    rec[:, u, j, :], None).then_inc(s_sc[u], 16)

            @block.vector
            def _(v):
                chain = [0]

                def link(ins):
                    chain[0] += 1
                    ins.then_inc(s_chain, 1)
                    v.wait_ge(s_chain, chain[0])

                v.memset(zero[:, :], 0.0).then_inc(s_c, 1)
                link(v.memset(hot[:, 1, :, :], 0.0))
                v.wait_ge(s_src, 16)
                link(v.tensor_single_scalar(part_i[:, :], src_i[:, :], 7, op=ALU.logical_shift_right))
                link(v.tensor_copy(hi[:, :], part_i[:, :]))
                link(v.tensor_single_scalar(src_i[:, :], src_i[:, :], P - 1, op=ALU.bitwise_and))
                link(v.tensor_copy(lo, src_i[:, :]))
                v.wait_ge(s_c, 5)

                def one_hot(n, u):
                    return v.tensor_tensor(hot[:, u, :, :], hi[:, bass.ds(n * COLS, COLS)].unsqueeze(2).to_broadcast([P, COLS, NB]),
                                           iota_b[:, :].unsqueeze(1).to_broadcast([P, COLS, NB]), ALU.is_equal)

                with v.Fori(0, STEPS // 2) as i:
                    for u in range(2):
                        n = i * 2 + u
                        v.wait_ge(s_used, n + 1)
                        one_hot(n, u).then_inc(s_hot, 1)
                v.wait_ge(s_used, STEPS + 2)
                link(v.tensor_copy(tot[:, :, :].rearrange("p (g j) b -> p g (j b)", g=4), ps[:, 0:4, 0:HW]))
                link(v.tensor_reduce(cnt[:, 0, :], tot[:, :, :].rearrange("p c b -> p b c"), AX.X, ALU.add))
                link(v.tensor_scalar(cnt[:, 1, :], cnt[:, 0, :], float(GROUP * P - 1), None, ALU.add))
                link(v.tensor_copy(cnt_i[:, :], cnt[:, 1, :]))
                link(v.tensor_single_scalar(cnt_i[:, :], cnt_i[:, :], 8, op=ALU.logical_shift_right))
                link(v.tensor_single_scalar(cnt_i[:, :], cnt_i[:, :], 8, op=ALU.logical_shift_left))
                link(v.tensor_copy(cnt[:, 1, :], cnt_i[:, :]))
                link(v.memset(cnt[:, 2, :], 1.0))
                link(v.tensor_tensor_scan(cnt[:, 3, :], cnt[:, 2, :], cnt[:, 1, :], 0.0, ALU.mult, ALU.add))
                link(v.tensor_tensor(base[:, 0, :], cnt[:, 3, :], cnt[:, 1, :], ALU.subtract))
                for j in range(1, COLS):
                    link(v.tensor_tensor(base[:, j, :], base[:, j - 1, :], tot[:, j - 1, :], ALU.add))
                v.memset(hot[:, 1, :, :], 0.0).then_inc(s_base, 1)
                link(v.tensor_tensor(cmp[:, :, :], cnt[:, 3, :].unsqueeze(1).to_broadcast([P, GC, NB]),
                                     gval[:, :].unsqueeze(2).to_broadcast([P, GC, NB]), ALU.is_le))
                link(v.tensor_reduce(blk_f[:, :], cmp[:, :, :], AX.X, ALU.add))
                link(v.tensor_scalar(blk_f[:, :], blk_f[:, :], float(NB - 1), None, ALU.min))
                v.tensor_copy(blk_i[:, :], blk_f[:, :]).then_inc(s_blk, 1)

                def rank(i):
                    for u in range(2):
                        n = i * 2 + u
                        one_hot(n, u).then_inc(s_hot2, 1)
                        for g in range(4):
                            v.wait_ge(s_rank, n * 4 + g + 1)
                            v.tensor_tensor(prod[:, 4 * g:4 * g + 4, :], hot[:, u, 4 * g:4 * g + 4, :],
                                            ps[:, g, 0:HW].rearrange("p (j b) -> p j b", j=4), ALU.mult).then_inc(s_prod, 1)
                        v.wait_ge(s_prod, n * 4 + 4)
                        v.tensor_reduce(pos_f[:, u, :], prod[:, :, :], AX.X, ALU.add).then_inc(s_red, 1)
                        v.wait_ge(s_red, n + 1)
                        wait(v, s_sc[u], i * (16 * COLS))
                        v.tensor_copy(pos[:, u, :], pos_f[:, u, :]).then_inc(s_pos, 1)
                        v.wait_ge(s_rec[u], i * 16 + 16)
                        v.tensor_copy(rec[:, u, :, LO_AT:LO_AT + 1], lo[:, bass.ds(n * COLS, COLS)].unsqueeze(2)).then_inc(s_lo, 1)
                looped(v, STEPS // 2, rank)

            @block.tensor
            def _(pe):
                pe.wait_ge(s_c, 5)
                for g in range(4):
                    last = pe.matmul(ps[:, g, 0:HW], ones[:, :], zero[:, :], start=True, stop=False, skip_group_check=True)
                last.then_inc(s_used, 2)
                with pe.Fori(0, STEPS // 2) as i:
                    for u in range(2):
                        pe.wait_ge(s_hot, i * 2 + u + 1)
                        for g in range(4):
                            last = pe.matmul(ps[:, g, 0:HW], ones[:, :],
                                             hot[:, u, 4 * g:4 * g + 4, :].rearrange("p j b -> p (j b)"), start=False, stop=False, skip_group_check=True)
                        last.then_inc(s_used, 1)
                pe.wait_ge(s_base, 1)
                for g in range(4):
                    last = pe.matmul(ps[:, g, 0:HW], ident[:, :], base[:, 4 * g:4 * g + 4, :].rearrange("p j b -> p (j b)"),
                                     start=True, stop=False, skip_group_check=True)

                def rank(i):
                    for u in range(2):
                        n = i * 2 + u
                        pe.wait_ge(s_hot2, n + 1)
                        wait(pe, s_prod, n * 4)
                        for g in range(4):
                            pe.matmul(ps[:, g, 0:HW], rest[:, :], hot[:, 1 - u, 4 * g:4 * g + 4, :].rearrange("p j b -> p (j b)"),
                                      start=False, stop=False, skip_group_check=True)
                            pe.matmul(ps[:, g, 0:HW], below[:, :], hot[:, u, 4 * g:4 * g + 4, :].rearrange("p j b -> p (j b)"),
                                      start=False, stop=False, skip_group_check=True).then_inc(s_rank, 1)
                looped(pe, STEPS // 2, rank)

        with ExitStack() as st:
            we = sb("we", [P, CH * D], stack=st)
            w2 = sb("w2", [P, D], stack=st)
            b2 = sb("b2", [1, D], stack=st)
            one_row = sb("one_row", [1, P], stack=st)
            rec = sb("rec_l0", [P, RING, CH, WORDS], stack=st)
            gat = sb("gat_l0", [P, RING, CH, D], stack=st)
            hot = sb("hot_l0", [P, RING, CH, P], stack=st)
            hot_b = sb("hot_b", [P, 2, CH, P], bf16, stack=st)
            hotT = sb("hotT", [P, 2, CH, P], bf16, stack=st)
            ident_b = sb("ident_b", [P, P], bf16, stack=st)
            recT = sb("recT", [P, 2, P], stack=st)
            hid = sb("hid", [P, 2, CH, P], stack=st)
            msg = sb("msg", [P, 2, CH, D], stack=st)
            ps = st.enter_context(nc.psum_tensor("ps2", [P, 8, 512], f32))
            ps_b = [ps[:, c, 0:256].bitcast(bf16) for c in range(2)]
            s_w, s_zero = sem("e_weights"), sem("e_zeroed")
            s_rec = [sem(f"e_rec{r}") for r in range(RING)]
            s_gat = [sem(f"e_gathered{r}") for r in range(RING)]
            s_hot, s_tp, s_cp, s_z = sem("e_hot"), sem("e_transposed"), sem("e_copied"), sem("e_pre1")
            s_hid, s_mp, s_m, s_ag, s_add = sem("e_hid"), sem("e_pre2"), sem("e_msg"), sem("e_group_sums"), sem("e_added")
            s_turn, s_load_turn = sem("e_turn"), sem("e_load_turn")
            rec_v = recs.rearrange("(k g p a) w -> k p g (a w)", g=CH // GROUP, p=P, a=GROUP)
            block = st.enter_context(nc.Block())

            @block.sync
            def _(sp):
                sp.dma_start(we[:, :], w_edge).then_inc(s_w, 16)
                sp.dma_start(w2[:, :], e_w2).then_inc(s_w, 16)
                sp.dma_start(b2[:, :], e_b2).then_inc(s_w, 16)

                def load(i, r):
                    k = i * RING + r
                    wait(sp, s_tp, k - RING + 1)
                    sp.sem_inc(s_load_turn, 1)
                    wait(sp, s_gat[r], i * (16 * CH))
                    src_ap = rec_v[bass.ds(k, 1), :, :, :].rearrange("k p g w -> (k p) g w")
                    sp.dma_start(rec[:, r, :, :].rearrange("p (g a) w -> p g (a w)", a=GROUP), src_ap).then_inc(s_rec[r], 16)
                looped(sp, CHUNKS // RING, lambda i: [load(i, r) for r in range(RING)])

            @block.gpsimd
            def _(pool):
                def gather(i, r):
                    k = i * RING + r
                    pool.wait_ge(s_rec[r], i * 16 + 16)
                    pool.sem_inc(s_turn, 1)
                    if not isinstance(i, int) or i > 0:
                        pool.wait_ge(s_z, k - RING + 1)
                        pool.sem_inc(s_turn, 1)
                    for t in range(CH):
                        pool.indirect_dma_start(gat[:, r, t, :], None, dst_tab,
                                                bass.IndirectOffsetOnAxis(ap=rec[:, r, t, DST_AT:DST_AT + 1].bitcast(i32), axis=0)).then_inc(s_gat[r], 16)
                looped(pool, CHUNKS // RING, lambda i: [gather(i, r) for r in range(RING)])

            @block.vector
            def _(v):
                v.memset(one_row[:, :], 1.0).then_inc(s_zero, 1)
                v.tensor_copy(ident_b[:, :], ident[:, :]).then_inc(s_zero, 1)
                v.memset(big_b[:, :, :], 0.0).then_inc(s_zero, 1)
                v.wait_ge(s_zero, 3)

                def one_hot(k, i, r):
                    v.wait_ge(s_rec[r], i * 16 + 16)
                    wait(v, s_ag, k - RING + 1)
                    v.tensor_tensor(hot[:, r, :, :], rec[:, r, :, LO_AT:LO_AT + 1].to_broadcast([P, CH, P]),
                                    iota_n[:, :].unsqueeze(1).to_broadcast([P, CH, P]), ALU.is_equal).then_inc(s_hot, 1)
                    v.wait_ge(s_hot, k * 2 + 1)
                    wait(v, s_tp, k - 1)
                    v.tensor_copy(hot_b[:, r % 2, :, :], hot[:, r, :, :]).then_inc(s_hot, 1)

                def add(k, r):
                    for g in range(CH // GROUP):
                        b = v.value_load(blk_row[0:1, bass.ds(k * 2 + g, 1)], min_val=0, max_val=NB - 1)
                        into = big_b[:, bass.ds(b, 1), :].rearrange("p a f -> p (a f)")
                        v.wait_ge(s_ag, k + 1)
                        wait(v, s_add, k * 2 + g)
                        v.tensor_tensor(into, into, ps[:, 5 + r % 2, g * D:(g + 1) * D], ALU.add).then_inc(s_add, 1)

                def chunk(i):
                    for r in range(RING):
                        k = i * RING + r
                        one_hot(k, i, r)
                        if not (isinstance(k, int) and k == 0):
                            add(k - 1, (r - 1) % RING)
                looped(v, CHUNKS // RING, chunk)
                add(CHUNKS - 1, RING - 1)

            @block.scalar
            def _(act):
                def copies(k, r):
                    act.wait_ge(s_tp, k + 1)
                    act.activation(hotT[:, r % 2, :, :].rearrange("p t e -> p (t e)"), ps_b[r % 2], ACT.Copy).then_inc(s_cp, 1)
                    act.activation(recT[:, r % 2, :], ps[:, 2, (r % 2) * P:(r % 2 + 1) * P], ACT.Copy).then_inc(s_cp, 1)

                def silu_msg(k, r):
                    act.wait_ge(s_mp, k + 1)
                    wait(act, s_ag, k - 1)
                    act.activation(msg[:, r % 2, :, :].rearrange("p t e -> p (t e)"), ps[:, 4, :], ACT.Silu).then_inc(s_m, 1)

                def silu_hid(k, r):
                    act.wait_ge(s_z, k + 1)
                    act.activation(hid[:, r % 2, :, :].rearrange("p t e -> p (t e)"), ps[:, 3, :], ACT.Silu).then_inc(s_hid, 1)

                def chunk(i):
                    for r in range(RING):
                        k = i * RING + r
                        copies(k, r)
                        if not (isinstance(k, int) and k == 0):
                            silu_msg(k - 1, (r - 1) % RING)
                        silu_hid(k, r)
                looped(act, CHUNKS // RING, chunk)
                silu_msg(CHUNKS - 1, RING - 1)

            @block.tensor
            def _(pe):
                pe.wait_ge(s_w, 48)
                pe.wait_ge(s_zero, 3)

                def transposes(k, i, r):
                    pe.wait_ge(s_hot, k * 2 + 2)
                    for t in range(CH):
                        pe.transpose(ps_b[r % 2][:, t * P:(t + 1) * P], hot_b[:, r % 2, t, :], ident_b[:, :])
                    pe.wait_ge(s_rec[r], i * 16 + 16)
                    pe.transpose(ps[:, 2, (r % 2) * P:(r % 2 + 1) * P], rec[:, r, :, :].rearrange("p t w -> p (t w)"),
                                 ident[:, :]).then_inc(s_tp, 1)

                def pre1(k, i, r):
                    bs = [pe.value_load(blk_row[0:1, bass.ds(k * 2 + g, 1)], min_val=0, max_val=NB - 1) for g in range(2)]
                    pe.wait_ge(s_cp, k * 2 + 2)
                    pe.wait_ge(s_gat[r], i * (16 * CH) + 16 * CH)
                    for g in range(CH // GROUP):
                        cols = slice(g * GROUP * P, (g + 1) * GROUP * P)
                        for s in range(3):
                            pe.matmul(ps[:, 3, cols], src_tab[:, bass.ds(bs[g], 1), s, :].rearrange("p a f -> p (a f)"),
                                      hotT[:, r % 2, GROUP * g:GROUP * (g + 1), :].rearrange("p t e -> p (t e)"), start=(s == 0), stop=False,
                                      skip_group_check=True)
                        for t in range(GROUP * g, GROUP * (g + 1)):
                            pe.matmul(ps[:, 3, t * P:(t + 1) * P], gat[:, r, t, :], ident[:, :], start=False, stop=False, skip_group_check=True)
                            last = pe.matmul(ps[:, 3, t * P:(t + 1) * P], we[:, t * D:(t + 1) * D], recT[:, r % 2, :],
                                             start=False, stop=True, skip_group_check=True)
                    last.then_inc(s_z, 1)

                def pre2(k, r):
                    pe.wait_ge(s_hid, k + 1)
                    for t in range(CH):
                        pe.matmul(ps[:, 4, t * D:(t + 1) * D], hid[:, r % 2, t, :], w2[:, :], start=True, stop=False)
                        last = pe.matmul(ps[:, 4, t * D:(t + 1) * D], one_row[:, :], b2[:, :], start=False, stop=True)
                    last.then_inc(s_mp, 1)

                def sums(k, r):
                    pe.wait_ge(s_m, k + 1)
                    wait(pe, s_add, (k - 1) * 2)
                    for t in range(CH):
                        g = t // GROUP
                        last = pe.matmul(ps[:, 5 + r % 2, g * D:(g + 1) * D], hot[:, r, t, :], msg[:, r % 2, t, :],
                                         start=(t % GROUP == 0), stop=(t % GROUP == GROUP - 1))
                    last.then_inc(s_ag, 1)

                def chunk(i):
                    for r in range(RING):
                        k = i * RING + r
                        first = isinstance(k, int) and k == 0
                        transposes(k, i, r)
                        if not first:
                            pre2(k - 1, (r - 1) % RING)
                        pre1(k, i, r)
                        if not first:
                            sums(k - 1, (r - 1) % RING)
                looped(pe, CHUNKS // RING, chunk)
                pre2(CHUNKS - 1, RING - 1)
                sums(CHUNKS - 1, RING - 1)

        with ExitStack() as st:
            wu = sb("wu", [P, 3 * D], stack=st)
            bu = sb("bu", [P, D], stack=st)
            nd = sb("nd", [P, 2, 4, 2 * D], stack=st)
            sums0 = sb("sums0", [P, 4, D], stack=st)
            t1 = sb("t1", [P, 4, P], stack=st)
            u1 = sb("u1", [P, 4, D], stack=st)
            u2 = sb("u2", [P, 4, D], stack=st)
            t2 = sb("t2", [P, 4, P], stack=st)
            x1 = sb("x1", [P, 2, 4, D], stack=st)
            h2 = sb("h2", [P, 4, D], stack=st)
            t3 = sb("t3", [P, 4, P], stack=st)
            hop = sb("hop", [P, 2, 4, D], stack=st)
            stats = sb("stats2", [P, 4, 6], stack=st)
            mv = sb("mv2", [P, 4, 2], stack=st)
            sd = sb("sd2", [P, 4], stack=st)
            rstd = sb("rstd2", [P, 4], stack=st)
            nmr = sb("nmr2", [P, 4], stack=st)
            ps = st.enter_context(nc.psum_tensor("ps3", [P, 8, 512], f32))
            s_w = sem("u_weights")
            s_nd = [sem("u_nodes0"), sem("u_nodes1")]
            s_pe, s_t, s_u1, s_u2 = sem("u_products"), sem("u_copied"), sem("u_part"), sem("u_silu")
            s_x1, s_st, s_mv, s_rs, s_nm, s_h2, s_hop = (sem("u_x1"), sem("u_stats"), sem("u_mean_var"), sem("u_rstd"),
                                                         sem("u_shift"), sem("u_h2"), sem("u_hop"))
            s_turn2, s_sd2, s_turn_v2 = sem('u_turn'), sem('u_std'), sem('u_turn_v')
            s_xa = sem("u_x1_part")
            s_out = [sem("u_stored0"), sem("u_stored1")]
            nod_v = node_dr.rearrange("(b p) f -> p b f", p=P)
            x1_v = x1_dr.rearrange("(b p) f -> p b f", p=P)
            hop_v = hop_tab.rearrange("(b p) f -> p b f", p=P)
            block = st.enter_context(nc.Block())

            @block.sync
            def _(sp):
                sp.dma_start(wu[:, :], w_update).then_inc(s_w, 16)
                sp.dma_start(bu[:, :], n_b2.partition_broadcast(P)).then_inc(s_w, 16)

                def quads(i):
                    for u in range(2):
                        wait(sp, s_x1, (i * 2 + u) - 1)
                        sp.dma_start(nd[:, u, :, :], nod_v[:, bass.ds(i * 8 + 4 * u, 4), :]).then_inc(s_nd[u], 16)
                looped(sp, NQ // 2, quads)

            @block.gpsimd
            def _(pool):
                def quads(i):
                    for u in range(2):
                        n = i * 2 + u
                        pool.wait_ge(s_x1, n + 1)
                        pool.sem_inc(s_turn2, 1)
                        pool.dma_start(x1_v[:, bass.ds(i * 8 + 4 * u, 4), :], x1[:, u, :, :]).then_inc(s_out[u], 16)
                        pool.wait_ge(s_hop, n + 1)
                        pool.sem_inc(s_turn2, 1)
                        pool.dma_start(hop_v[:, bass.ds(i * 8 + 4 * u, 4), :], hop[:, u, :, :]).then_inc(s_out[u], 16)
                looped(pool, NQ // 2, quads)
                for u in range(2):
                    pool.wait_ge(s_out[u], NQ // 2 * 32)

            @block.vector
            def _(v):
                v.wait_ge(s_w, 32)

                def quads(i):
                    for u in range(2):
                        n = i * 2 + u
                        v.wait_ge(s_nd[u], i * 16 + 16)
                        v.wait_ge(s_pe, n * 6 + 2)
                        v.tensor_tensor(u1[:, :, :], ps[:, 1, :].rearrange("p (t f) -> p t f", t=4), nd[:, u, :, 0:D], ALU.add).then_inc(s_u1, 1)
                        v.wait_ge(s_pe, n * 6 + 4)
                        wait(v, s_out[u], i * 32)
                        v.tensor_tensor(x1[:, u, :, :], ps[:, 3, :].rearrange("p (t f) -> p t f", t=4), nd[:, u, :, D:2 * D], ALU.add).then_inc(s_xa, 1)
                        v.wait_ge(s_xa, n + 1)
                        v.tensor_tensor(x1[:, u, :, :], x1[:, u, :, :], bu[:, :].unsqueeze(1).to_broadcast([P, 4, D]), ALU.add).then_inc(s_x1, 1)
                        v.wait_ge(s_x1, n + 1)
                        for t in range(4):
                            v.bn_stats(stats[:, t, :], x1[:, u, t, :]).then_inc(s_st, 1)
                        v.wait_ge(s_st, n * 4 + 4)
                        v.sem_inc(s_turn_v2, 1)
                        for t in range(4):
                            v.bn_aggr(mv[:, t, :], stats[:, t, :]).then_inc(s_mv, 1)
                        v.wait_ge(s_sd2, n + 1)
                        v.reciprocal(rstd[:, :], sd[:, :]).then_inc(s_rs, 1)
                        v.wait_ge(s_rs, n + 1)
                        v.scalar_tensor_tensor(out=nmr[:, :], in0=mv[:, :, 0], scalar=-1.0, in1=rstd[:, :],
                                               op0=ALU.mult, op1=ALU.mult).then_inc(s_nm, 1)
                        v.wait_ge(s_pe, n * 6 + 6)
                        v.tensor_copy(hop[:, u, :, :], ps[:, 5, :].rearrange("p (t f) -> p t f", t=4)).then_inc(s_hop, 1)
                looped(v, NQ // 2, quads)

            @block.scalar
            def _(act):
                def quads(i):
                    for u in range(2):
                        n = i * 2 + u
                        act.activation(sums0[:, :, :], big_b[:, bass.ds(n * 4, 4), :], ACT.Copy).then_inc(s_t, 1)
                        act.wait_ge(s_pe, n * 6 + 1)
                        act.activation(t1[:, :, :].rearrange("p t n -> p (t n)"), ps[:, 0, :], ACT.Copy).then_inc(s_t, 1)
                        act.wait_ge(s_u1, n + 1)
                        act.activation(u2[:, :, :], u1[:, :, :], ACT.Silu).then_inc(s_u2, 1)
                        act.wait_ge(s_pe, n * 6 + 3)
                        act.activation(t2[:, :, :].rearrange("p t n -> p (t n)"), ps[:, 2, :], ACT.Copy).then_inc(s_t, 1)
                        act.wait_ge(s_mv, n * 4 + 4)
                        act.activation(sd[:, :], mv[:, :, 1], ACT.Sqrt, bias=eps[:, :]).then_inc(s_sd2, 1)
                        act.wait_ge(s_nm, n + 1)
                        for t in range(4):
                            act.activation(h2[:, t, :], x1[:, u, t, :], ACT.Relu, bias=nmr[:, t:t + 1],
                                           scale=rstd[:, t:t + 1]).then_inc(s_h2, 1)
                        act.wait_ge(s_pe, n * 6 + 5)
                        act.activation(t3[:, :, :].rearrange("p t n -> p (t n)"), ps[:, 4, :], ACT.Copy).then_inc(s_t, 1)
                looped(act, NQ // 2, quads)

            @block.tensor
            def _(pe):
                pe.wait_ge(s_w, 32)

                def transposed(bank, rows):
                    for t in range(4):
                        last = pe.transpose(ps[:, bank, t * P:(t + 1) * P], rows(t), ident[:, :])
                    last.then_inc(s_pe, 1)

                def products(bank, lhsT, w):
                    for t in range(4):
                        last = pe.matmul(ps[:, bank, t * D:(t + 1) * D], lhsT[:, t, :], wu[:, w * D:(w + 1) * D], start=True, stop=True)
                    last.then_inc(s_pe, 1)

                def quads(i):
                    for u in range(2):
                        n = i * 2 + u
                        pe.wait_ge(s_t, n * 4 + 1)
                        transposed(0, lambda t: sums0[:, t, :])
                        pe.wait_ge(s_t, n * 4 + 2)
                        products(1, t1, 0)
                        pe.wait_ge(s_u2, n + 1)
                        transposed(2, lambda t: u2[:, t, :])
                        pe.wait_ge(s_t, n * 4 + 3)
                        products(3, t2, 1)
                        pe.wait_ge(s_h2, n * 4 + 4)
                        transposed(4, lambda t: h2[:, t, :])
                        pe.wait_ge(s_t, n * 4 + 4)
                        wait(pe, s_hop, n)
                        products(5, t3, 2)
                looped(pe, NQ // 2, quads)

        def hop_pass(name, table, width, ones_at, into_tile):
            cols = into_tile.shape[2]
            with ExitStack() as st:
                rec = sb(name + "_rec", [P, RING, CH, WORDS], stack=st)
                gat = sb(name + "_gat", [P, RING, CH, 2 * FO + 4], stack=st)
                hot = sb(name + "_hot", [P, RING, CH, P], stack=st)
                ps = st.enter_context(nc.psum_tensor(name + "_ps", [P, 8, 512], f32))
                s_rec = [sem(f"{name}_recs{r}") for r in range(RING)]
                s_gat = [sem(f"{name}_gathered{r}") for r in range(RING)]
                s_hot, s_ag, s_add, s_zero, s_turn = (sem(name + "_hots"), sem(name + "_group_sums"), sem(name + "_added"),
                                                      sem(name + "_zeroed"), sem(name + "_turn"))
                s_load_turn = sem(name + "_load_turn")
                rec_v = recs.rearrange("(k g p a) w -> k p g (a w)", g=CH // GROUP, p=P, a=GROUP)
                block = st.enter_context(nc.Block())

                @block.sync
                def _(sp):
                    def load(i, r):
                        k = i * RING + r
                        wait(sp, s_hot, (k - RING + 1) * CH)
                        sp.sem_inc(s_load_turn, 1)
                        wait(sp, s_gat[r], i * (16 * CH))
                        src_ap = rec_v[bass.ds(k, 1), :, :, :].rearrange("k p g w -> (k p) g w")
                        sp.dma_start(rec[:, r, :, :].rearrange("p (g a) w -> p g (a w)", a=GROUP), src_ap).then_inc(s_rec[r], 16)
                    looped(sp, CHUNKS // RING, lambda i: [load(i, r) for r in range(RING)])

                @block.gpsimd
                def _(pool):
                    if ones_at is not None:
                        pool.memset(gat[:, :, :, ones_at:ones_at + 1], 1.0).then_inc(s_zero, 1)

                    def gather(i, r):
                        k = i * RING + r
                        pool.wait_ge(s_rec[r], i * 16 + 16)
                        pool.sem_inc(s_turn, 1)
                        if not isinstance(i, int) or i > 0:
                            pool.wait_ge(s_ag, k - RING + 1)
                            pool.sem_inc(s_turn, 1)
                        for t in range(CH):
                            pool.indirect_dma_start(gat[:, r, t, 0:width], None, table,
                                                    bass.IndirectOffsetOnAxis(ap=rec[:, r, t, DST_AT:DST_AT + 1].bitcast(i32), axis=0)).then_inc(s_gat[r], 16)
                    looped(pool, CHUNKS // RING, lambda i: [gather(i, r) for r in range(RING)])

                @block.vector
                def _(v):
                    v.memset(into_tile, 0.0).then_inc(s_zero, 1)
                    v.wait_ge(s_zero, 2 if ones_at is not None else 1)

                    def one_hot(k, i, r):
                        v.wait_ge(s_rec[r], i * 16 + 16)
                        wait(v, s_ag, k - RING + 1)
                        for t in range(CH):
                            v.tensor_scalar(hot[:, r, t, :], iota_n[:, :], rec[:, r, t, LO_AT:LO_AT + 1], rec[:, r, t, W_AT:W_AT + 1],
                                            ALU.is_equal, ALU.mult).then_inc(s_hot, 1)

                    def add(k, r):
                        for g in range(CH // GROUP):
                            b = v.value_load(blk_row[0:1, bass.ds(k * 2 + g, 1)], min_val=0, max_val=NB - 1)
                            into = into_tile[:, bass.ds(b, 1), :].rearrange("p a f -> p (a f)")
                            v.wait_ge(s_ag, k + 1)
                            wait(v, s_add, k * 2 + g)
                            v.tensor_tensor(into, into, ps[:, r, g * 256:g * 256 + cols], ALU.add).then_inc(s_add, 1)

                    def chunk(i):
                        for r in range(RING):
                            k = i * RING + r
                            one_hot(k, i, r)
                            if not (isinstance(k, int) and k == 0):
                                add(k - 1, (r - 1) % RING)
                    looped(v, CHUNKS // RING, chunk)
                    add(CHUNKS - 1, RING - 1)

                @block.tensor
                def _(pe):
                    pe.wait_ge(s_zero, 2 if ones_at is not None else 1)

                    def sums(i, r):
                        k = i * RING + r
                        pe.wait_ge(s_hot, k * CH + CH)
                        pe.wait_ge(s_gat[r], i * (16 * CH) + 16 * CH)
                        wait(pe, s_add, (k - RING + 1) * 2)
                        for t in range(CH):
                            g = t // GROUP
                            last = pe.matmul(ps[:, r, g * 256:g * 256 + cols], hot[:, r, t, :], gat[:, r, t, 0:cols],
                                             start=(t % GROUP == 0), stop=(t % GROUP == GROUP - 1))
                        last.then_inc(s_ag, 1)
                    looped(pe, CHUNKS // RING, lambda i: [sums(i, r) for r in range(RING)])

        sums1 = big_a[:, :, 0:2 * FO + 1]
        hop_pass("f", hop_tab, 2 * FO, 2 * FO, sums1)
        with ExitStack() as st:
            s_t2 = sem("t2_stored")
            block = st.enter_context(nc.Block())

            @block.sync
            def _(sp):
                sp.dma_start(hop2_tab.rearrange("(b p) w -> p b w", p=P), big_a[:, :, FO:2 * FO + 1]).then_inc(s_t2, 16)
                sp.wait_ge(s_t2, 16)
        sums2 = big_b[:, :, 0:FO + 1]
        hop_pass("g", hop2_tab, FO + 1, None, sums2)

        with ExitStack() as st:
            BL = 8
            NT = NB // BL
            bh = sb("bh", [P, 2, FO], stack=st)
            fcs = sb("fcs", [P, 2, FO], stack=st)
            bfs = sb("bfs", [P, 2], stack=st)
            xr = sb("xr", [P, BL, D], stack=st)
            res = sb("res", [P, BL, D], stack=st)
            y = sb("y", [P, BL, FO], stack=st)
            z = sb("z", [P, BL, FO], stack=st)
            mask = sb("mask", [P, BL], stack=st)
            inv = sb("inv", [P, BL], stack=st)
            gate = sb("gate", [P, BL], stack=st)
            s_w, s_x, s_g, s_gs, s_out = sem("o_weights"), sem("o_x1"), sem("o_gate"), sem("o_sigmoid"), sem("o_stored")
            s_y, s_res, s_rows = sem("o_chain"), sem("o_added"), sem("o_rows")
            x1_v = x1_dr.rearrange("(b p) f -> p b f", p=P)
            out_v = out.rearrange("(b p) f -> p b f", p=P)
            block = st.enter_context(nc.Block())
            LINKS = 9

            @block.sync
            def _(sp):
                sp.dma_start(bh[:, :, :].rearrange("p a b -> p (a b)"), b_hop.partition_broadcast(P)).then_inc(s_w, 16)
                sp.dma_start(fcs[:, :, :].rearrange("p a b -> p (a b)"), fc.partition_broadcast(P)).then_inc(s_w, 16)
                sp.dma_start(bfs[:, :], bf.partition_broadcast(P)).then_inc(s_w, 16)

                def tiles(i):
                    wait(sp, s_res, i * 2)
                    sp.dma_start(xr[:, :, :], x1_v[:, bass.ds(i * BL, BL), :]).then_inc(s_x, 16)
                    sp.wait_ge(s_res, i * 2 + 2)
                    sp.dma_start(out_v[:, bass.ds(i * BL, BL), :], res[:, :, :]).then_inc(s_out, 16)
                looped(sp, NT, tiles)
                sp.wait_ge(s_out, NT * 16)

            @block.vector
            def _(v):
                v.wait_ge(s_w, 48)

                def tiles(i):
                    v.wait_ge(s_x, i * 16 + 16)
                    for hop in range(2):
                        n = i * 2 + hop
                        done = [0]

                        def link(ins):
                            done[0] += 1
                            ins.then_inc(s_y, 1)
                            v.wait_ge(s_y, n * LINKS + done[0])

                        big, deg_at = (big_a, 2 * FO) if hop == 0 else (big_b, FO)
                        deg = big[:, bass.ds(i * BL, BL), deg_at:deg_at + 1].rearrange("p b o -> p (b o)")
                        agg = big[:, bass.ds(i * BL, BL), 0:FO]
                        link(v.tensor_single_scalar(mask[:, :], deg, 0.0, op=ALU.is_gt))
                        link(v.tensor_tensor(inv[:, :], deg, mask[:, :], ALU.mult))
                        link(v.scalar_tensor_tensor(out=inv[:, :], in0=inv[:, :], scalar=1.0, in1=mask[:, :], op0=ALU.add, op1=ALU.subtract))
                        link(v.reciprocal(inv[:, :], inv[:, :]))
                        link(v.tensor_tensor(inv[:, :], inv[:, :], mask[:, :], ALU.mult))
                        link(v.tensor_tensor(y[:, :, :], agg, inv[:, :].unsqueeze(2).to_broadcast([P, BL, FO]), ALU.mult))
                        link(v.tensor_tensor(y[:, :, :], y[:, :, :], bh[:, hop, :].unsqueeze(1).to_broadcast([P, BL, FO]), ALU.add))
                        link(v.tensor_tensor(z[:, :, :], y[:, :, :], fcs[:, hop, :].unsqueeze(1).to_broadcast([P, BL, FO]), ALU.mult))
                        v.tensor_reduce(gate[:, :], z[:, :, :], AX.X, ALU.add).then_inc(s_g, 1)
                        v.wait_ge(s_gs, n + 1)
                        link(v.scalar_tensor_tensor(out=z[:, :, :], in0=y[:, :, :], scalar=0.0, in1=gate[:, :].unsqueeze(2).to_broadcast([P, BL, FO]),
                                                    op0=ALU.min, op1=ALU.mult))
                        v.scalar_tensor_tensor(out=z[:, :, :], in0=y[:, :, :], scalar=0.0, in1=z[:, :, :],
                                               op0=ALU.max, op1=ALU.add).then_inc(s_rows, 1)
                        v.wait_ge(s_rows, n + 1)
                        if hop == 0:
                            wait(v, s_out, i * 16)
                        v.tensor_tensor(res[:, :, hop * FO:(hop + 1) * FO], z[:, :, :], xr[:, :, hop * FO:(hop + 1) * FO],
                                        ALU.add).then_inc(s_res, 1)
                looped(v, NT, tiles)

            @block.scalar
            def _(act):
                act.wait_ge(s_w, 48)

                def tiles(i):
                    for hop in range(2):
                        act.wait_ge(s_g, i * 2 + hop + 1)
                        act.activation(gate[:, :], gate[:, :], ACT.Sigmoid, bias=bfs[:, hop:hop + 1]).then_inc(s_gs, 1)
                looped(act, NT, tiles)


def kernel(x, src, dst, edge_attr_16, edge_weight, L0_gnn_eW1, L0_gnn_eb1, L0_gnn_eW2, L0_gnn_eb2, L0_gnn_nW1,
           L0_gnn_nb1, L0_gnn_nW2, L0_gnn_nb2, L1_gnn_W0, L1_gnn_b0, L1_gnn_W1, L1_gnn_b1, L1_gnn_fc0, L1_gnn_bf0,
           L1_gnn_fc1, L1_gnn_bf1):
    import numpy as np
    import concourse.bacc as bacc
    from concourse import mybir as mb
    from concourse.bass_utils import run_bass_kernel_spmd as run

    x, src, dst, attr, weight = map(np.asarray, (x, src, dst, edge_attr_16, edge_weight))
    eW1, nW1 = np.asarray(L0_gnn_eW1), np.asarray(L0_gnn_nW1)
    n, e = x.shape[0], src.shape[0]
    blocks, cols, _ = sizes(n, e)
    x_pad = np.zeros((blocks * P, D), np.float32)
    x_pad[:n] = x
    src_pad = np.full(P * cols, blocks * P - 1, np.int32)
    src_pad[:e] = src
    edges = np.zeros((P * cols, WORDS), np.float32)
    edges[:e, :DE] = attr
    edges[:e, W_AT] = weight
    edges.view(np.int32)[:e, DST_AT] = dst
    w_edge = np.zeros((P, CH, D), np.float32)
    for t in range(CH):
        w_edge[t * WORDS:t * WORDS + DE, t] = eW1[2 * D:]
    row = lambda *parts: np.concatenate([np.asarray(p).reshape(-1) for p in parts])
    ins = {
        "x": x_pad, "src": src_pad.reshape(P, cols), "edges": edges,
        "w_node": np.concatenate([eW1[:D], eW1[D:2 * D], nW1[:D]], axis=1),
        "b_node": row(L0_gnn_eb1, np.zeros(D, np.float32), L0_gnn_nb1),
        "w_edge": w_edge.reshape(P, CH * D), "e_w2": np.asarray(L0_gnn_eW2),
        "e_b2": np.asarray(L0_gnn_eb2).reshape(1, D),
        "w_update": np.concatenate([nW1[D:], np.asarray(L0_gnn_nW2), np.asarray(L1_gnn_W0), np.asarray(L1_gnn_W1)], axis=1),
        "n_b2": row(L0_gnn_nb2), "b_hop": row(L1_gnn_b0, L1_gnn_b1), "fc": row(L1_gnn_fc0, L1_gnn_fc1),
        "bf": row(L1_gnn_bf0, L1_gnn_bf1),
    }
    ins = {k: np.ascontiguousarray(v) for k, v in ins.items()}
    nc = bacc.Bacc("TRN2", target_bir_lowering=False, num_devices=1)
    args = [nc.dram_tensor("in_" + k, v.shape, mb.dt.from_np(v.dtype), kind="ExternalInput").ap() for k, v in ins.items()]
    out = nc.dram_tensor("out", (blocks * P, D), mb.dt.float32, kind="ExternalOutput").ap()
    gnn(nc, *args, out)
    r = run(nc, [{"in_" + k: v for k, v in ins.items()}], core_ids=[0])
    return r.results[0]["out"][:n]
```

```python
from contextlib import ExitStack

import concourse.bass as bass
from concourse import mybir

P = 128
D = 128
DE = 16
FO = 64
IN_WORDS = 20
W_IN, DST_IN = 16, 17
WORDS = 32
PART_WORDS = 3 * DE // 2
W_AT, LO_AT, DST_AT = 24, 25, 26
STACK = 8 * DE
CH = 4
RING = 4
COLS = 16
EPS = 1e-5


def up(a, b):
    return (a + b - 1) // b * b


def wait(eng, s, value):
    if not isinstance(value, int) or value > 0:
        eng.wait_ge(s, value)


def looped(eng, steps, body):
    body(0)
    with eng.Fori(1, steps) as i:
        body(i)


def looped_to_last(eng, steps, body):
    body(0)
    with eng.Fori(1, steps - 1) as i:
        body(i)
    body(steps - 1)


def sizes(n_nodes, n_edges):
    return up(n_nodes + 1, 8 * P) // P, up(up(n_edges, P) // P, 2 * COLS)


def gnn(nc, x, src, edges, w_node, b_node, w_edge, e_w2, e_b2, w_update, n_b2, b_hop, fc, bf, out):
    f32, bf16, i32 = mybir.dt.float32, mybir.dt.bfloat16, mybir.dt.int32
    ALU, ACT, AX = mybir.AluOpType, mybir.ActivationFunctionType, mybir.AxisListType
    NB = x.shape[0] // P
    C = src.shape[1]
    SLOTS = up(P * C + NB * (P - 1), RING * CH * P)
    TILES = SLOTS // P
    GC = up(TILES, P) // P
    CHUNKS = TILES // CH
    NQ = NB // 4
    STEPS = C // COLS
    HW = NB // 4 * COLS
    assert HW <= 512 and NB % 8 == 0 and C % (2 * COLS) == 0 and CHUNKS % RING == 0 and NB < STEPS

    recs = nc.dram_tensor("recs", [SLOTS, WORDS], f32).ap()
    dst_tab = nc.dram_tensor("dst_tab", [NB * P, 3 * D], bf16).ap()
    node_dr = nc.dram_tensor("node_dr", [NB * P, 2 * D], f32).ap()
    blk_dr = nc.dram_tensor("blk_dr", [GC * P], i32).ap()
    hop_tab = nc.dram_tensor("hop_tab", [NB * P, 2 * FO], f32).ap()
    x1_dr = nc.dram_tensor("x1_dr", [NB * P, D], f32).ap()
    hop2_tab = nc.dram_tensor("hop2_tab", [NB * P, FO + 1], f32).ap()

    ctx = ExitStack()
    with ctx:
        def sb(name, shape, dt=f32, stack=ctx):
            return stack.enter_context(nc.sbuf_tensor(name, shape, dt))

        def sem(name):
            return ctx.enter_context(nc.semaphore(name))

        big_a = sb("big_a", [P, NB, 3 * D // 2])
        big_b = sb("big_b", [P, NB, D])
        src_tab = big_a[:, :, :].bitcast(bf16).rearrange("p b (s f) -> p b s f", s=3)
        ident = sb("ident", [P, P])
        iota_n = sb("iota_n", [P, P])
        eps = sb("eps", [P, 1])
        blk_row = sb("blk_row", [1, GC * P], i32)

        def tile_blocks(eng, first, n):
            _, blocks = nc.values_load_multi_w_load_instructions(
                blk_row[0:1, bass.ds(first, n)], engines=[eng.engine], min_val=0, max_val=NB - 1,
                skip_runtime_bounds_check_because="the table was clamped to the blocks' numbers")
            return list(blocks)

        with ExitStack() as st:
            spare = big_b[:, :, :].rearrange("p b f -> p (b f)")
            at = [0]

            def from_spare(words):
                at[0] += words
                assert at[0] <= NB * D
                return spare[:, at[0] - words:at[0]]

            src_i = from_spare(C).bitcast(i32)
            lo = from_spare(C)
            cmp = from_spare(GC * NB).rearrange("p (c b) -> p c b", b=NB)
            base = from_spare(NB * COLS).rearrange("p (b c) -> p b c", c=COLS)
            hi = sb("hi", [P, C], bf16, stack=st)
            iota_b = sb("iota_b", [P, NB, COLS], bf16, stack=st)
            ones = sb("ones", [P, P], bf16, stack=st)
            below = sb("below", [P, P], bf16, stack=st)
            rest = sb("rest", [P, P], bf16, stack=st)
            zero = sb("zero", [P, HW], bf16, stack=st)
            hot = sb("hot", [P, 2, NB, COLS], bf16, stack=st)
            prod = sb("prod", [P, NB, COLS], stack=st)
            tot = prod
            pos_f = sb("pos_f", [P, 2, COLS], stack=st)
            pos = sb("pos", [P, 2, COLS], i32, stack=st)
            edge = sb("edge", [P, 2, COLS, IN_WORDS], stack=st)
            rec = sb("rec", [P, 2, COLS, WORDS], stack=st)
            fill = sb("fill", [P, 16, WORDS], stack=st)
            cnt = sb("cnt", [P, 4, NB], stack=st)
            cnt_i = sb("cnt_i", [P, NB], i32, stack=st)
            gval = sb("gval", [P, GC], stack=st)
            blk_f = sb("blk_f", [P, GC], stack=st)
            blk_i = sb("blk_i", [P, GC], i32, stack=st)
            wn = sb("wn", [P, 3 * D], stack=st)
            bn = sb("bn", [P, 3 * D], stack=st)
            xn = sb("xn", [P, 2, D], stack=st)
            h = sb("h", [P, 2, D], stack=st)
            hT = sb("hT", [P, 2, P], stack=st)
            tmp = sb("tmp", [P, 2, 2, D], stack=st)
            dst_st = sb("dst_st", [P, 2, 3, D], bf16, stack=st)
            node_st = sb("node_st", [P, 2, 2, D], stack=st)
            stats = sb("stats", [P, 2, 6], stack=st)
            mv = sb("mv", [P, 2, 2], stack=st)
            sd = sb("sd", [P, 2], stack=st)
            rstd = sb("rstd", [P, 2], stack=st)
            nmr = sb("nmr", [P, 2], stack=st)
            ps = st.enter_context(nc.psum_tensor("ps1", [P, 8, 512], f32))
            s_src, s_fill, s_fz, s_c, s_chain = sem("s_src"), sem("s_filled"), sem("s_fill_ready"), sem("s_consts"), sem("s_chain")
            s_hot, s_used, s_rank, s_prod = sem("s_hot"), sem("s_hot_counted"), sem("s_ranked"), sem("s_prod")
            s_pos, s_base, s_blk, s_blk_st = sem("s_pos"), sem("s_base"), sem("s_blk"), sem("s_blk_stored")
            s_edge = [sem("s_edge0"), sem("s_edge1")]
            s_sp, s_built = sem("s_split"), sem("s_built")
            s_sc = [sem("s_scattered0"), sem("s_scattered1")]
            s_turn, s_z, s_hot2 = sem("s_turn"), sem("s_z"), sem("s_hot2")
            s_red = sem("s_reduced")
            s_w, s_id, s_eps, s_x = sem("n_weights"), sem("n_ident"), sem("n_eps"), sem("n_x")
            s_st, s_mv, s_sd, s_rs, s_nm = sem("n_stats"), sem("n_mean_var"), sem("n_std"), sem("n_rstd"), sem("n_shift")
            s_h, s_tp, s_hT, s_mm = sem("n_h"), sem("n_hT_psum"), sem("n_hT"), sem("n_products")
            s_ev, s_nsp, s_nst, s_turn_v, s_turn_a = sem("n_evacuated"), sem("n_split"), sem("n_stored"), sem("n_turn_v"), sem("n_turn_a")
            e_v = edges.rearrange("(p c) w -> p c w", p=P)
            fill_v = recs.rearrange("(n p a) w -> n p (a w)", p=P, a=16)
            NF = fill_v.shape[0]
            x_v = x.rearrange("(b p) f -> p b f", p=P)
            tab_v = dst_tab.rearrange("(b p) f -> p b f", p=P)
            nod_v = node_dr.rearrange("(b p) f -> p b f", p=P)
            NP2 = NB // 2
            block = st.enter_context(nc.Block())

            def with_nodes(eng, step, node):
                def both(i):
                    step(i)
                    node(i)
                both(0)
                with eng.Fori(1, NP2) as i:
                    both(i)
                with eng.Fori(NP2, STEPS // 2) as i:
                    step(i)

            @block.sync
            def _(sp):
                sp.dma_start(src_i, src).then_inc(s_src, 16)
                sp.dma_start(wn[:, :], w_node).then_inc(s_w, 16)
                sp.dma_start(bn[:, :], b_node.partition_broadcast(P)).then_inc(s_w, 16)
                sp.wait_ge(s_fz, 1)
                with sp.Fori(0, NF) as i:
                    sp.dma_start(fill_v[bass.ds(i, 1), :, :].rearrange("a p w -> (a p) w"),
                                 fill[:, :, :].rearrange("p a w -> p (a w)")).then_inc(s_fill, 16)

                def load(i):
                    for u in range(2):
                        wait(sp, s_built, (i * 2 + u - 1) * 4)
                        sp.dma_start(edge[:, u, :, :], e_v[:, bass.ds((i * 2 + u) * COLS, COLS), :]).then_inc(s_edge[u], 16)
                looped(sp, STEPS // 2, load)
                sp.wait_ge(s_blk, 1)
                sp.dma_start(blk_dr.rearrange("(p c) -> p c", p=P), blk_i[:, :]).then_inc(s_blk_st, 16)
                sp.wait_ge(s_blk_st, 16)
                sp.dma_start(blk_row[:, :], blk_dr.unsqueeze(0)).then_inc(s_blk_st, 16)
                sp.wait_ge(s_blk_st, 32)
                for u in range(2):
                    sp.wait_ge(s_sc[u], STEPS // 2 * 16 * COLS)

            @block.gpsimd
            def _(pool):
                pool.memset(fill[:, :, :], 0.0).then_inc(s_z, 1)
                pool.memset(ident[:, :], 0.0).then_inc(s_z, 1)
                pool.memset(rec[:, :, :, :], 0.0).then_inc(s_z, 1)
                pool.memset(ones[:, :], 1.0).then_inc(s_z, 1)
                pool.wait_ge(s_z, 4)
                pool.memset(fill[:, :, LO_AT:LO_AT + 1], -1.0).then_inc(s_fz, 1)
                pool.affine_select(out=below[:, :], in_=ones[:, :], compare_op=ALU.is_gt, fill=0.0,
                                   base=0, pattern=[[1, P]], channel_multiplier=-1).then_inc(s_c, 1)
                pool.affine_select(out=rest[:, :], in_=ones[:, :], compare_op=ALU.is_ge, fill=0.0,
                                   base=0, pattern=[[-1, P]], channel_multiplier=1).then_inc(s_c, 1)
                pool.affine_select(out=ident[:, :], in_=ident[:, :], compare_op=ALU.not_equal, fill=1.0,
                                   base=0, pattern=[[-1, P]], channel_multiplier=1).then_inc(s_c, 1)
                pool.iota(iota_b[:, :, :], [[1, NB], [0, COLS]], 0, 0, allow_small_or_imprecise_dtypes=True).then_inc(s_c, 1)
                pool.iota(iota_n[:, :], [[1, P]], 0, 0, allow_small_or_imprecise_dtypes=True).then_inc(s_c, 1)
                pool.iota(gval[:, :], [[P, GC]], 0, P * GC, allow_small_or_imprecise_dtypes=True).then_inc(s_c, 1)
                pool.wait_ge(s_fill, NF * 16)
                with pool.Fori(0, STEPS // 2) as i:
                    for u in range(2):
                        pool.wait_ge(s_pos, i * 2 + u + 1)
                        pool.sem_inc(s_turn, 1)
                        pool.wait_ge(s_built, (i * 2 + u) * 4 + 4)
                        pool.sem_inc(s_turn, 1)
                        for j in range(COLS):
                            pool.indirect_dma_start(recs, bass.IndirectOffsetOnAxis(ap=pos[:, u, j:j + 1], axis=0),
                                                    rec[:, u, j, :], None).then_inc(s_sc[u], 16)

            @block.vector
            def _(v):
                chain = [0]

                def link(ins):
                    chain[0] += 1
                    ins.then_inc(s_chain, 1)
                    v.wait_ge(s_chain, chain[0])

                v.memset(zero[:, :], 0.0).then_inc(s_id, 1)
                v.memset(eps[:, :], EPS).then_inc(s_eps, 1)
                link(v.memset(hot[:, 1, :, :], 0.0))
                v.wait_ge(s_src, 16)
                link(v.tensor_single_scalar(lo.bitcast(i32), src_i, 7, op=ALU.logical_shift_right))
                link(v.tensor_copy(hi[:, :], lo.bitcast(i32)))
                link(v.tensor_single_scalar(src_i, src_i, P - 1, op=ALU.bitwise_and))
                link(v.tensor_copy(lo, src_i))
                v.wait_ge(s_c, 6)

                def one_hot(n, u):
                    return v.tensor_tensor(hot[:, u, :, :], hi[:, bass.ds(n * COLS, COLS)].unsqueeze(1).to_broadcast([P, NB, COLS]),
                                           iota_b[:, :, :], ALU.is_equal)

                with v.Fori(0, STEPS // 2) as i:
                    for u in range(2):
                        n = i * 2 + u
                        v.wait_ge(s_used, n + 1)
                        one_hot(n, u).then_inc(s_hot, 1)
                v.wait_ge(s_used, STEPS + 2)
                link(v.tensor_copy(tot[:, :, :].rearrange("p (g b) c -> p g (b c)", g=4), ps[:, 0:4, 0:HW]))
                link(v.tensor_reduce(cnt[:, 0, :], tot[:, :, :], AX.X, ALU.add))
                link(v.tensor_scalar(cnt[:, 1, :], cnt[:, 0, :], float(P - 1), None, ALU.add))
                link(v.tensor_copy(cnt_i[:, :], cnt[:, 1, :]))
                link(v.tensor_single_scalar(cnt_i[:, :], cnt_i[:, :], 7, op=ALU.logical_shift_right))
                link(v.tensor_single_scalar(cnt_i[:, :], cnt_i[:, :], 7, op=ALU.logical_shift_left))
                link(v.tensor_copy(cnt[:, 1, :], cnt_i[:, :]))
                link(v.memset(cnt[:, 2, :], 1.0))
                link(v.tensor_tensor_scan(cnt[:, 3, :], cnt[:, 2, :], cnt[:, 1, :], 0.0, ALU.mult, ALU.add))
                link(v.tensor_tensor(base[:, :, 0], cnt[:, 3, :], cnt[:, 1, :], ALU.subtract))
                for j in range(1, COLS):
                    link(v.tensor_tensor(base[:, :, j], base[:, :, j - 1], tot[:, :, j - 1], ALU.add))
                v.memset(hot[:, 1, :, :], 0.0).then_inc(s_base, 1)
                link(v.tensor_tensor(cmp, cnt[:, 3, :].unsqueeze(1).to_broadcast([P, GC, NB]),
                                     gval[:, :].unsqueeze(2).to_broadcast([P, GC, NB]), ALU.is_le))
                link(v.tensor_reduce(blk_f[:, :], cmp, AX.X, ALU.add))
                link(v.tensor_scalar(blk_f[:, :], blk_f[:, :], float(NB - 1), None, ALU.min))
                v.tensor_copy(blk_i[:, :], blk_f[:, :]).then_inc(s_blk, 1)

                def rank(i):
                    for u in range(2):
                        n = i * 2 + u
                        one_hot(n, u).then_inc(s_hot2, 1)
                        v.wait_ge(s_edge[u], i * 16 + 16)
                        wait(v, s_sc[u], i * (16 * COLS))
                        parts = rec[:, u, :, 0:PART_WORDS].bitcast(bf16).rearrange("p c (s f) -> p c s f", s=3)
                        rem = edge[:, u, :, 0:DE]
                        for s in range(3):
                            v.tensor_copy(parts[:, :, s, :], rem).then_inc(s_sp if s < 2 else s_built, 1)
                            if s < 2:
                                v.wait_ge(s_sp, n * 4 + 2 * s + 1)
                                v.tensor_tensor(rem, rem, parts[:, :, s, :], ALU.subtract).then_inc(s_sp, 1)
                                v.wait_ge(s_sp, n * 4 + 2 * s + 2)
                        v.tensor_copy(rec[:, u, :, W_AT:W_AT + 1], edge[:, u, :, W_IN:W_IN + 1]).then_inc(s_built, 1)
                        v.tensor_copy(rec[:, u, :, DST_AT:DST_AT + 1].bitcast(i32), edge[:, u, :, DST_IN:DST_IN + 1].bitcast(i32)).then_inc(s_built, 1)
                        v.tensor_copy(rec[:, u, :, LO_AT:LO_AT + 1], lo[:, bass.ds(n * COLS, COLS)].unsqueeze(2)).then_inc(s_built, 1)
                        v.wait_ge(s_rank, n + 1)
                        v.tensor_tensor(prod[:, :, :].rearrange("p (g b) c -> p g (b c)", g=4), hot[:, u, :, :].rearrange("p (g b) c -> p g (b c)", g=4),
                                        ps[:, 0:4, 0:HW], ALU.mult).then_inc(s_prod, 1)
                        v.wait_ge(s_prod, n + 1)
                        v.tensor_reduce(pos_f[:, u, :], prod[:, :, :].rearrange("p b c -> p c b"), AX.X, ALU.add).then_inc(s_red, 1)
                        v.wait_ge(s_red, n + 1)
                        v.tensor_copy(pos[:, u, :], pos_f[:, u, :]).then_inc(s_pos, 1)

                def node(i):
                    v.wait_ge(s_x, i * 16 + 16)
                    for t in range(2):
                        v.bn_stats(stats[:, t, :], xn[:, t, :]).then_inc(s_st, 1)
                    v.wait_ge(s_st, i * 2 + 2)
                    v.sem_inc(s_turn_v, 1)
                    for t in range(2):
                        v.bn_aggr(mv[:, t, :], stats[:, t, :]).then_inc(s_mv, 1)
                    v.wait_ge(s_sd, i + 1)
                    v.reciprocal(rstd[:, :], sd[:, :]).then_inc(s_rs, 1)
                    v.wait_ge(s_rs, i + 1)
                    v.scalar_tensor_tensor(out=nmr[:, :], in0=mv[:, :, 0], scalar=-1.0, in1=rstd[:, :],
                                           op0=ALU.mult, op1=ALU.mult).then_inc(s_nm, 1)
                    wait(v, s_nst, i * 32)
                    v.wait_ge(s_h, i * 2 + 2)
                    v.tensor_tensor(node_st[:, :, 1, :], xn[:, :, :], h[:, :, :], ALU.add).then_inc(s_ev, 1)
                    v.wait_ge(s_mm, i + 1)
                    v.tensor_tensor(tmp[:, :, :, :].rearrange("p t s f -> p t (s f)"), ps[:, 5:7, 0:2 * D],
                                    bn[:, 0:2 * D].unsqueeze(1).to_broadcast([P, 2, 2 * D]), ALU.add).then_inc(s_ev, 1)
                    v.tensor_tensor(node_st[:, :, 0, :], ps[:, 5:7, 2 * D:3 * D],
                                    bn[:, 2 * D:3 * D].unsqueeze(1).to_broadcast([P, 2, D]), ALU.add).then_inc(s_ev, 1)
                    v.wait_ge(s_ev, i * 3 + 2)
                    for s in range(3):
                        for side, part in enumerate((src_tab[:, bass.ds(i * 2, 2), s, :], dst_st[:, :, s, :])):
                            v.tensor_copy(part, tmp[:, :, side, :]).then_inc(s_nsp, 1)
                        v.wait_ge(s_nsp, i * 10 + 4 * s + 2)
                        if s < 2:
                            for side, part in enumerate((src_tab[:, bass.ds(i * 2, 2), s, :], dst_st[:, :, s, :])):
                                v.tensor_tensor(tmp[:, :, side, :], tmp[:, :, side, :], part, ALU.subtract).then_inc(s_nsp, 1)
                            v.wait_ge(s_nsp, i * 10 + 4 * s + 4)
                with_nodes(v, rank, node)

            @block.scalar
            def _(act):
                act.wait_ge(s_eps, 1)

                def node(i):
                    wait(act, s_ev, i * 3)
                    act.dma_start(xn[:, :, :], x_v[:, bass.ds(i * 2, 2), :]).then_inc(s_x, 16)
                    act.wait_ge(s_mv, i * 2 + 2)
                    act.activation(sd[:, :], mv[:, :, 1], ACT.Sqrt, bias=eps[:, :]).then_inc(s_sd, 1)
                    act.wait_ge(s_nm, i + 1)
                    for t in range(2):
                        act.activation(h[:, t, :], xn[:, t, :], ACT.Relu, bias=nmr[:, t:t + 1], scale=rstd[:, t:t + 1]).then_inc(s_h, 1)
                    act.wait_ge(s_tp, i + 1)
                    act.activation(hT[:, :, :].rearrange("p a b -> p (a b)"), ps[:, 4, 0:2 * P], ACT.Copy).then_inc(s_hT, 1)
                    act.wait_ge(s_nsp, i * 10 + 10)
                    act.sem_inc(s_turn_a, 1)
                    act.wait_ge(s_ev, i * 3 + 3)
                    act.dma_start(tab_v[:, bass.ds(i * 2, 2), :], dst_st[:, :, :, :].rearrange("p t s f -> p t (s f)")).then_inc(s_nst, 16)
                    act.dma_start(nod_v[:, bass.ds(i * 2, 2), :], node_st[:, :, :, :].rearrange("p t s f -> p t (s f)")).then_inc(s_nst, 16)
                looped(act, NP2, node)
                act.wait_ge(s_nst, NP2 * 32)

            @block.tensor
            def _(pe):
                pe.wait_ge(s_c, 6)
                pe.wait_ge(s_id, 1)

                def quarter(u, g):
                    return hot[:, u, g * NB // 4:(g + 1) * NB // 4, :].rearrange("p b c -> p (b c)")

                for g in range(4):
                    last = pe.matmul(ps[:, g, 0:HW], ones[:, :], zero[:, :], start=True, stop=False, skip_group_check=True)
                last.then_inc(s_used, 2)
                with pe.Fori(0, STEPS // 2) as i:
                    for u in range(2):
                        pe.wait_ge(s_hot, i * 2 + u + 1)
                        for g in range(4):
                            last = pe.matmul(ps[:, g, 0:HW], ones[:, :], quarter(u, g), start=False, stop=False, skip_group_check=True)
                        last.then_inc(s_used, 1)
                pe.wait_ge(s_base, 1)
                for g in range(4):
                    pe.matmul(ps[:, g, 0:HW], ident[:, :], base[:, g * NB // 4:(g + 1) * NB // 4, :].rearrange("p b c -> p (b c)"),
                              start=True, stop=False, skip_group_check=True)
                pe.wait_ge(s_w, 32)

                def rank(i):
                    for u in range(2):
                        n = i * 2 + u
                        pe.wait_ge(s_hot2, n + 1)
                        wait(pe, s_prod, n)
                        for g in range(4):
                            pe.matmul(ps[:, g, 0:HW], rest[:, :], quarter(1 - u, g), start=False, stop=False, skip_group_check=True)
                            last = pe.matmul(ps[:, g, 0:HW], below[:, :], quarter(u, g), start=False, stop=False, skip_group_check=True)
                        last.then_inc(s_rank, 1)

                def node(i):
                    pe.wait_ge(s_h, i * 2 + 2)
                    for t in range(2):
                        last = pe.transpose(ps[:, 4, t * P:(t + 1) * P], h[:, t, :], ident[:, :])
                    last.then_inc(s_tp, 1)
                    pe.wait_ge(s_hT, i + 1)
                    wait(pe, s_ev, i * 3)
                    for t in range(2):
                        last = pe.matmul(ps[:, 5 + t, 0:3 * D], hT[:, t, :], wn[:, :], start=True, stop=True)
                    last.then_inc(s_mm, 1)
                with_nodes(pe, rank, node)

        with ExitStack() as st:
            w_f = sb("w_f", [P, 2, D], stack=st)
            w_part = sb("w_part", [P, 3, 2, D], bf16, stack=st)
            we = sb("we", [P, D], bf16, stack=st)
            w2 = sb("w2", [P, D], stack=st)
            b2 = sb("b2", [P, CH, D], bf16, stack=st)
            ones = sb("ones_l0", [P, P], bf16, stack=st)
            ident_b = sb("ident_b", [P, P], bf16, stack=st)
            rec = sb("rec_l0", [P, RING, CH, WORDS], stack=st)
            gat = sb("gat_l0", [P, RING, CH, 3, D], bf16, stack=st)
            dup = sb("dup", [P, 2, CH, STACK], bf16, stack=st)
            hot = sb("hot_l0", [P, RING, CH, P], stack=st)
            hot_b = sb("hot_b", [P, 2, CH, P], bf16, stack=st)
            hotT = sb("hotT", [P, 2, CH * P], bf16, stack=st)
            featT = sb("featT", [STACK, 2, CH * P], bf16, stack=st)
            hid = sb("hid", [P, 2, CH * P], stack=st)
            msg = sb("msg", [P, 2, CH * D], stack=st)
            ps = st.enter_context(nc.psum_tensor("ps2", [P, 8, 512], f32))
            hotT_ps = [ps[:, c, 0:256].bitcast(bf16) for c in range(2)]
            featT_ps = [ps[:, 7, 256 * c:256 * c + 256].bitcast(bf16) for c in range(2)]
            PRE1, PRE2, SUMS = 2, 3, 4
            s_w, s_zero, s_wp = sem("e_weights"), sem("e_zeroed"), sem("e_weight_parts")
            s_rec = [sem(f"e_rec{r}") for r in range(RING)]
            s_gat = [sem(f"e_gathered{r}") for r in range(RING)]
            s_hot, s_tp, s_cp, s_z = sem("e_hot"), sem("e_transposed"), sem("e_copied"), sem("e_pre1")
            s_hid, s_mp, s_m, s_ag, s_add = sem("e_hid"), sem("e_pre2"), sem("e_msg"), sem("e_tile_sums"), sem("e_added")
            s_turn, s_load_turn = sem("e_turn"), sem("e_load_turn")
            rec_v = recs.rearrange("(k t p) w -> k p t w", t=CH, p=P)
            ZEROED = 4 + 6 + 1
            HOTS = 5
            block = st.enter_context(nc.Block())

            @block.sync
            def _(sp):
                sp.dma_start(w_f[:, 0, :], w_edge).then_inc(s_w, 16)
                sp.dma_start(w_f[:, 1, :], e_b2.partition_broadcast(P)).then_inc(s_w, 16)
                sp.dma_start(w2[:, :], e_w2).then_inc(s_w, 16)

                def load(i, r):
                    k = i * RING + r
                    wait(sp, s_tp, k - RING + 1)
                    sp.sem_inc(s_load_turn, 1)
                    wait(sp, s_gat[r], i * (16 * CH))
                    sp.dma_start(rec[:, r, :, :], rec_v[bass.ds(k, 1), :, :, :].rearrange("k p t w -> (k p) t w")).then_inc(s_rec[r], 16)
                looped(sp, CHUNKS // RING, lambda i: [load(i, r) for r in range(RING)])

            @block.gpsimd
            def _(pool):
                def gather(i, r):
                    k = i * RING + r
                    pool.wait_ge(s_rec[r], i * 16 + 16)
                    pool.sem_inc(s_turn, 1)
                    if not isinstance(i, int) or i > 0:
                        pool.wait_ge(s_z, k - RING + 1)
                        pool.sem_inc(s_turn, 1)
                    for t in range(CH):
                        pool.indirect_dma_start(gat[:, r, t, :, :].rearrange("p s f -> p (s f)"), None, dst_tab,
                                                bass.IndirectOffsetOnAxis(ap=rec[:, r, t, DST_AT:DST_AT + 1].bitcast(i32), axis=0)).then_inc(s_gat[r], 16)
                looped(pool, CHUNKS // RING, lambda i: [gather(i, r) for r in range(RING)])

            @block.vector
            def _(v):
                zeroed = [0]

                def begun(ins):
                    zeroed[0] += 1
                    ins.then_inc(s_zero, 1)

                begun(v.memset(dup[:, :, :, :], 0.0))
                begun(v.memset(b2[:, :, :], 0.0))
                begun(v.memset(ones[:, :], 1.0))
                begun(v.tensor_copy(ident_b[:, :], ident[:, :]))
                v.wait_ge(s_zero, 4)

                def one_hot(k, i, r):
                    v.wait_ge(s_rec[r], i * 16 + 16)
                    wait(v, s_ag, k - RING + 1)
                    v.tensor_tensor(hot[:, r, :, :], rec[:, r, :, LO_AT:LO_AT + 1].to_broadcast([P, CH, P]),
                                    iota_n[:, :].unsqueeze(1).to_broadcast([P, CH, P]), ALU.is_equal).then_inc(s_hot, 1)
                    wait(v, s_tp, k - 1)
                    parts = rec[:, r, :, 0:PART_WORDS].bitcast(bf16)
                    for at, n in ((0, 3), (4, 2), (6, 1)):
                        v.tensor_copy(dup[:, r % 2, :, at * DE:(at + n) * DE], parts[:, :, 0:n * DE]).then_inc(s_hot, 1)
                    v.wait_ge(s_hot, k * HOTS + 1)
                    v.tensor_copy(hot_b[:, r % 2, :, :], hot[:, r, :, :]).then_inc(s_hot, 1)

                def add(k, r, blocks):
                    v.wait_ge(s_ag, k + 1)
                    for t in range(CH):
                        into = big_b[:, bass.ds(blocks[t], 1), :].rearrange("p a f -> p (a f)")
                        wait(v, s_add, k * CH + t)
                        v.tensor_tensor(into, into, ps[:, SUMS + r % 2, t * D:(t + 1) * D], ALU.add).then_inc(s_add, 1)

                def chunk(i):
                    first, last = isinstance(i, int) and i == 0, isinstance(i, int) and i > 0
                    skip = CH if first else 0
                    blocks = [None] * skip + tile_blocks(v, i * (RING * CH) - CH + skip, RING * CH - skip)
                    for r in range(RING):
                        k = i * RING + r
                        if not (last and r == RING - 1):
                            one_hot(k + 1, i + (r + 1) // RING, (r + 1) % RING)
                        if not (first and r == 0):
                            add(k - 1, (r - 1) % RING, blocks[r * CH:(r + 1) * CH])

                one_hot(0, 0, 0)
                v.wait_ge(s_w, 48)
                for s in range(3):
                    v.tensor_copy(w_part[:, s, :, :], w_f[:, :, :]).then_inc(s_wp, 1)
                    v.wait_ge(s_wp, 2 * s + 1)
                    v.tensor_tensor(w_f[:, :, :], w_f[:, :, :], w_part[:, s, :, :], ALU.subtract).then_inc(s_wp, 1)
                    v.wait_ge(s_wp, 2 * s + 2)
                for s, (a, b) in enumerate(((0, 64), (64, 96), (96, 128))):
                    begun(v.tensor_copy(we[a:b, :], w_part[a:b, s, 0, :]))
                    begun(v.tensor_copy(b2[32 * s:32 * s + 1, :, :], w_part[32 * s:32 * s + 1, s, 1:2, :].to_broadcast([1, CH, D])))
                begun(v.memset(big_b[:, :, :], 0.0))
                v.wait_ge(s_zero, ZEROED)
                looped_to_last(v, CHUNKS // RING, chunk)
                add(CHUNKS - 1, RING - 1, tile_blocks(v, (CHUNKS - 1) * CH, CH))

            @block.scalar
            def _(act):
                def copies(k, r):
                    act.wait_ge(s_tp, k + 1)
                    act.activation(hotT[:, r % 2, :], hotT_ps[r % 2], ACT.Copy).then_inc(s_cp, 1)
                    act.activation(featT[:, r % 2, :], featT_ps[r % 2], ACT.Copy).then_inc(s_cp, 1)

                def silu_msg(k, r):
                    act.wait_ge(s_mp, k + 1)
                    wait(act, s_ag, k - 1)
                    act.activation(msg[:, r % 2, :], ps[:, PRE2, :], ACT.Silu).then_inc(s_m, 1)

                def silu_hid(k, r):
                    act.wait_ge(s_z, k + 1)
                    act.activation(hid[:, r % 2, :], ps[:, PRE1, :], ACT.Silu).then_inc(s_hid, 1)

                def chunk(i):
                    for r in range(RING):
                        k = i * RING + r
                        copies(k, r)
                        if not (isinstance(k, int) and k == 0):
                            silu_msg(k - 1, (r - 1) % RING)
                        silu_hid(k, r)
                looped(act, CHUNKS // RING, chunk)
                silu_msg(CHUNKS - 1, RING - 1)

            @block.tensor
            def _(pe):
                pe.wait_ge(s_w, 48)
                pe.wait_ge(s_zero, ZEROED)

                def transposes(k, r):
                    pe.wait_ge(s_hot, k * HOTS + HOTS)
                    for t in range(CH):
                        pe.transpose(hotT_ps[r % 2][:, t * P:(t + 1) * P], hot_b[:, r % 2, t, :], ident_b[:, :])
                    for t in range(CH):
                        last = pe.transpose(featT_ps[r % 2][:, t * P:(t + 1) * P], dup[:, r % 2, t, :], ident_b[:, :])
                    last.then_inc(s_tp, 1)

                def pre1(k, i, r, blocks):
                    pe.wait_ge(s_cp, k * 2 + 2)
                    pe.matmul(ps[:, PRE1, :], we[:, :], featT[:, r % 2, :], start=True, stop=False, skip_group_check=True)
                    for t in range(CH):
                        for s in range(3):
                            pe.matmul(ps[:, PRE1, t * P:(t + 1) * P], src_tab[:, bass.ds(blocks[t], 1), s, :].rearrange("p a f -> p (a f)"),
                                      hotT[:, r % 2, t * P:(t + 1) * P], start=False, stop=False, skip_group_check=True)
                    pe.wait_ge(s_gat[r], i * (16 * CH) + 16 * CH)
                    for t in range(CH):
                        for s in range(3):
                            last = pe.matmul(ps[:, PRE1, t * P:(t + 1) * P], gat[:, r, t, s, :], ident_b[:, :],
                                             start=False, stop=(s == 2), skip_group_check=True)
                    last.then_inc(s_z, 1)

                def pre2(k, r):
                    pe.wait_ge(s_hid, k + 1)
                    pe.matmul(ps[:, PRE2, :], ones[:, :], b2[:, :, :].rearrange("p t f -> p (t f)"), start=True, stop=False, skip_group_check=True)
                    for t in range(CH):
                        last = pe.matmul(ps[:, PRE2, t * D:(t + 1) * D], hid[:, r % 2, t * P:(t + 1) * P], w2[:, :], start=False, stop=True,
                                         skip_group_check=True)
                    last.then_inc(s_mp, 1)

                def sums(k, r):
                    pe.wait_ge(s_m, k + 1)
                    wait(pe, s_add, (k - 1) * CH)
                    for t in range(CH):
                        last = pe.matmul(ps[:, SUMS + r % 2, t * D:(t + 1) * D], hot[:, r, t, :], msg[:, r % 2, t * D:(t + 1) * D],
                                         start=True, stop=True)
                    last.then_inc(s_ag, 1)

                def chunk(i):
                    blocks = tile_blocks(pe, i * (RING * CH), RING * CH)
                    for r in range(RING):
                        k = i * RING + r
                        first = isinstance(k, int) and k == 0
                        transposes(k, r)
                        if not first:
                            pre2(k - 1, (r - 1) % RING)
                        pre1(k, i, r, blocks[r * CH:(r + 1) * CH])
                        if not first:
                            sums(k - 1, (r - 1) % RING)
                looped(pe, CHUNKS // RING, chunk)
                pre2(CHUNKS - 1, RING - 1)
                sums(CHUNKS - 1, RING - 1)

        with ExitStack() as st:
            wu = sb("wu", [P, 3 * D], stack=st)
            bu = sb("bu", [P, D], stack=st)
            nd = sb("nd", [P, 2, 4, 2 * D], stack=st)
            sums0 = sb("sums0", [P, 4, D], stack=st)
            t1 = sb("t1", [P, 4, P], stack=st)
            u1 = sb("u1", [P, 4, D], stack=st)
            u2 = sb("u2", [P, 4, D], stack=st)
            t2 = sb("t2", [P, 4, P], stack=st)
            x1 = sb("x1", [P, 2, 4, D], stack=st)
            h2 = sb("h2", [P, 4, D], stack=st)
            t3 = sb("t3", [P, 4, P], stack=st)
            hop = sb("hop", [P, 2, 4, D], stack=st)
            stats = sb("stats2", [P, 4, 6], stack=st)
            mv = sb("mv2", [P, 4, 2], stack=st)
            sd = sb("sd2", [P, 4], stack=st)
            rstd = sb("rstd2", [P, 4], stack=st)
            nmr = sb("nmr2", [P, 4], stack=st)
            ps = st.enter_context(nc.psum_tensor("ps3", [P, 8, 512], f32))
            s_w = sem("u_weights")
            s_nd = [sem("u_nodes0"), sem("u_nodes1")]
            s_pe, s_t, s_u1, s_u2 = sem("u_products"), sem("u_copied"), sem("u_part"), sem("u_silu")
            s_x1, s_st, s_mv, s_rs, s_nm, s_h2, s_hop = (sem("u_x1"), sem("u_stats"), sem("u_mean_var"), sem("u_rstd"),
                                                         sem("u_shift"), sem("u_h2"), sem("u_hop"))
            s_turn2, s_sd2, s_turn_v2 = sem('u_turn'), sem('u_std'), sem('u_turn_v')
            s_xa = sem("u_x1_part")
            s_out = [sem("u_stored0"), sem("u_stored1")]
            nod_v = node_dr.rearrange("(b p) f -> p b f", p=P)
            x1_v = x1_dr.rearrange("(b p) f -> p b f", p=P)
            hop_v = hop_tab.rearrange("(b p) f -> p b f", p=P)
            block = st.enter_context(nc.Block())

            @block.sync
            def _(sp):
                sp.dma_start(wu[:, :], w_update).then_inc(s_w, 16)
                sp.dma_start(bu[:, :], n_b2.partition_broadcast(P)).then_inc(s_w, 16)

                def quads(i):
                    for u in range(2):
                        wait(sp, s_x1, (i * 2 + u) - 1)
                        sp.dma_start(nd[:, u, :, :], nod_v[:, bass.ds(i * 8 + 4 * u, 4), :]).then_inc(s_nd[u], 16)
                looped(sp, NQ // 2, quads)

            @block.gpsimd
            def _(pool):
                def quads(i):
                    for u in range(2):
                        n = i * 2 + u
                        pool.wait_ge(s_x1, n + 1)
                        pool.sem_inc(s_turn2, 1)
                        pool.dma_start(x1_v[:, bass.ds(i * 8 + 4 * u, 4), :], x1[:, u, :, :]).then_inc(s_out[u], 16)
                        pool.wait_ge(s_hop, n + 1)
                        pool.sem_inc(s_turn2, 1)
                        pool.dma_start(hop_v[:, bass.ds(i * 8 + 4 * u, 4), :], hop[:, u, :, :]).then_inc(s_out[u], 16)
                looped(pool, NQ // 2, quads)
                for u in range(2):
                    pool.wait_ge(s_out[u], NQ // 2 * 32)

            @block.vector
            def _(v):
                v.wait_ge(s_w, 32)

                def quads(i):
                    for u in range(2):
                        n = i * 2 + u
                        v.wait_ge(s_nd[u], i * 16 + 16)
                        v.wait_ge(s_pe, n * 6 + 2)
                        v.tensor_tensor(u1[:, :, :], ps[:, 1, :].rearrange("p (t f) -> p t f", t=4), nd[:, u, :, 0:D], ALU.add).then_inc(s_u1, 1)
                        v.wait_ge(s_pe, n * 6 + 4)
                        wait(v, s_out[u], i * 32)
                        v.tensor_tensor(x1[:, u, :, :], ps[:, 3, :].rearrange("p (t f) -> p t f", t=4), nd[:, u, :, D:2 * D], ALU.add).then_inc(s_xa, 1)
                        v.wait_ge(s_xa, n + 1)
                        v.tensor_tensor(x1[:, u, :, :], x1[:, u, :, :], bu[:, :].unsqueeze(1).to_broadcast([P, 4, D]), ALU.add).then_inc(s_x1, 1)
                        v.wait_ge(s_x1, n + 1)
                        for t in range(4):
                            v.bn_stats(stats[:, t, :], x1[:, u, t, :]).then_inc(s_st, 1)
                        v.wait_ge(s_st, n * 4 + 4)
                        v.sem_inc(s_turn_v2, 1)
                        for t in range(4):
                            v.bn_aggr(mv[:, t, :], stats[:, t, :]).then_inc(s_mv, 1)
                        v.wait_ge(s_sd2, n + 1)
                        v.reciprocal(rstd[:, :], sd[:, :]).then_inc(s_rs, 1)
                        v.wait_ge(s_rs, n + 1)
                        v.scalar_tensor_tensor(out=nmr[:, :], in0=mv[:, :, 0], scalar=-1.0, in1=rstd[:, :],
                                               op0=ALU.mult, op1=ALU.mult).then_inc(s_nm, 1)
                        v.wait_ge(s_pe, n * 6 + 6)
                        v.tensor_copy(hop[:, u, :, :], ps[:, 5, :].rearrange("p (t f) -> p t f", t=4)).then_inc(s_hop, 1)
                looped(v, NQ // 2, quads)

            @block.scalar
            def _(act):
                def quads(i):
                    for u in range(2):
                        n = i * 2 + u
                        act.activation(sums0[:, :, :], big_b[:, bass.ds(n * 4, 4), :], ACT.Copy).then_inc(s_t, 1)
                        act.wait_ge(s_pe, n * 6 + 1)
                        act.activation(t1[:, :, :].rearrange("p t n -> p (t n)"), ps[:, 0, :], ACT.Copy).then_inc(s_t, 1)
                        act.wait_ge(s_u1, n + 1)
                        act.activation(u2[:, :, :], u1[:, :, :], ACT.Silu).then_inc(s_u2, 1)
                        act.wait_ge(s_pe, n * 6 + 3)
                        act.activation(t2[:, :, :].rearrange("p t n -> p (t n)"), ps[:, 2, :], ACT.Copy).then_inc(s_t, 1)
                        act.wait_ge(s_mv, n * 4 + 4)
                        act.activation(sd[:, :], mv[:, :, 1], ACT.Sqrt, bias=eps[:, :]).then_inc(s_sd2, 1)
                        act.wait_ge(s_nm, n + 1)
                        for t in range(4):
                            act.activation(h2[:, t, :], x1[:, u, t, :], ACT.Relu, bias=nmr[:, t:t + 1],
                                           scale=rstd[:, t:t + 1]).then_inc(s_h2, 1)
                        act.wait_ge(s_pe, n * 6 + 5)
                        act.activation(t3[:, :, :].rearrange("p t n -> p (t n)"), ps[:, 4, :], ACT.Copy).then_inc(s_t, 1)
                looped(act, NQ // 2, quads)

            @block.tensor
            def _(pe):
                pe.wait_ge(s_w, 32)

                def transposed(bank, rows):
                    for t in range(4):
                        last = pe.transpose(ps[:, bank, t * P:(t + 1) * P], rows(t), ident[:, :])
                    last.then_inc(s_pe, 1)

                def products(bank, lhsT, w):
                    for t in range(4):
                        last = pe.matmul(ps[:, bank, t * D:(t + 1) * D], lhsT[:, t, :], wu[:, w * D:(w + 1) * D], start=True, stop=True)
                    last.then_inc(s_pe, 1)

                def quads(i):
                    for u in range(2):
                        n = i * 2 + u
                        pe.wait_ge(s_t, n * 4 + 1)
                        transposed(0, lambda t: sums0[:, t, :])
                        pe.wait_ge(s_t, n * 4 + 2)
                        products(1, t1, 0)
                        pe.wait_ge(s_u2, n + 1)
                        transposed(2, lambda t: u2[:, t, :])
                        pe.wait_ge(s_t, n * 4 + 3)
                        products(3, t2, 1)
                        pe.wait_ge(s_h2, n * 4 + 4)
                        transposed(4, lambda t: h2[:, t, :])
                        pe.wait_ge(s_t, n * 4 + 4)
                        wait(pe, s_hop, n)
                        products(5, t3, 2)
                looped(pe, NQ // 2, quads)

        def hop_pass(name, table, width, ones_at, into_tile):
            cols = into_tile.shape[2]
            with ExitStack() as st:
                rec = sb(name + "_rec", [P, RING, CH, WORDS], stack=st)
                gat = sb(name + "_gat", [P, RING, CH, 2 * FO + 4], stack=st)
                hot = sb(name + "_hot", [P, RING, CH, P], stack=st)
                ps = st.enter_context(nc.psum_tensor(name + "_ps", [P, 8, 512], f32))
                s_rec = [sem(f"{name}_recs{r}") for r in range(RING)]
                s_gat = [sem(f"{name}_gathered{r}") for r in range(RING)]
                s_hot, s_ag, s_add, s_zero, s_turn = (sem(name + "_hots"), sem(name + "_group_sums"), sem(name + "_added"),
                                                      sem(name + "_zeroed"), sem(name + "_turn"))
                s_load_turn = sem(name + "_load_turn")
                rec_v = recs.rearrange("(k t p) w -> k p t w", t=CH, p=P)

                def bank(r, t):
                    return ps[:, 2 * r + t // 2, t % 2 * 256:t % 2 * 256 + cols]

                block = st.enter_context(nc.Block())

                @block.sync
                def _(sp):
                    def load(i, r):
                        k = i * RING + r
                        wait(sp, s_hot, (k - RING + 1) * CH)
                        sp.sem_inc(s_load_turn, 1)
                        wait(sp, s_gat[r], i * (16 * CH))
                        sp.dma_start(rec[:, r, :, :], rec_v[bass.ds(k, 1), :, :, :].rearrange("k p t w -> (k p) t w")).then_inc(s_rec[r], 16)
                    looped(sp, CHUNKS // RING, lambda i: [load(i, r) for r in range(RING)])

                @block.gpsimd
                def _(pool):
                    if ones_at is not None:
                        pool.memset(gat[:, :, :, ones_at:ones_at + 1], 1.0).then_inc(s_zero, 1)

                    def gather(i, r):
                        k = i * RING + r
                        pool.wait_ge(s_rec[r], i * 16 + 16)
                        pool.sem_inc(s_turn, 1)
                        if not isinstance(i, int) or i > 0:
                            pool.wait_ge(s_ag, k - RING + 1)
                            pool.sem_inc(s_turn, 1)
                        for t in range(CH):
                            pool.indirect_dma_start(gat[:, r, t, 0:width], None, table,
                                                    bass.IndirectOffsetOnAxis(ap=rec[:, r, t, DST_AT:DST_AT + 1].bitcast(i32), axis=0)).then_inc(s_gat[r], 16)
                    looped(pool, CHUNKS // RING, lambda i: [gather(i, r) for r in range(RING)])

                @block.vector
                def _(v):
                    v.memset(into_tile, 0.0).then_inc(s_zero, 1)
                    v.wait_ge(s_zero, 2 if ones_at is not None else 1)

                    def one_hot(k, i, r):
                        v.wait_ge(s_rec[r], i * 16 + 16)
                        wait(v, s_ag, k - RING + 1)
                        for t in range(CH):
                            v.tensor_scalar(hot[:, r, t, :], iota_n[:, :], rec[:, r, t, LO_AT:LO_AT + 1], rec[:, r, t, W_AT:W_AT + 1],
                                            ALU.is_equal, ALU.mult).then_inc(s_hot, 1)

                    def add(k, r, blocks):
                        v.wait_ge(s_ag, k + 1)
                        for t in range(CH):
                            into = into_tile[:, bass.ds(blocks[t], 1), :].rearrange("p a f -> p (a f)")
                            wait(v, s_add, k * CH + t)
                            v.tensor_tensor(into, into, bank(r, t), ALU.add).then_inc(s_add, 1)

                    def chunk(i):
                        first = isinstance(i, int)
                        skip = CH if first else 0
                        blocks = [None] * skip + tile_blocks(v, i * (RING * CH) - CH + skip, RING * CH - skip)
                        for r in range(RING):
                            k = i * RING + r
                            one_hot(k, i, r)
                            if not (first and r == 0):
                                add(k - 1, (r - 1) % RING, blocks[r * CH:(r + 1) * CH])
                    looped(v, CHUNKS // RING, chunk)
                    add(CHUNKS - 1, RING - 1, tile_blocks(v, (CHUNKS - 1) * CH, CH))

                @block.tensor
                def _(pe):
                    pe.wait_ge(s_zero, 2 if ones_at is not None else 1)

                    def sums(i, r):
                        k = i * RING + r
                        pe.wait_ge(s_hot, k * CH + CH)
                        pe.wait_ge(s_gat[r], i * (16 * CH) + 16 * CH)
                        wait(pe, s_add, (k - RING + 1) * CH)
                        for t in range(CH):
                            last = pe.matmul(bank(r, t), hot[:, r, t, :], gat[:, r, t, 0:cols], start=True, stop=True)
                        last.then_inc(s_ag, 1)
                    looped(pe, CHUNKS // RING, lambda i: [sums(i, r) for r in range(RING)])

        sums1 = big_a[:, :, 0:2 * FO + 1]
        hop_pass("f", hop_tab, 2 * FO, 2 * FO, sums1)
        with ExitStack() as st:
            s_t2 = sem("t2_stored")
            block = st.enter_context(nc.Block())

            @block.sync
            def _(sp):
                sp.dma_start(hop2_tab.rearrange("(b p) w -> p b w", p=P), big_a[:, :, FO:2 * FO + 1]).then_inc(s_t2, 16)
                sp.wait_ge(s_t2, 16)
        sums2 = big_b[:, :, 0:FO + 1]
        hop_pass("g", hop2_tab, FO + 1, None, sums2)

        with ExitStack() as st:
            BL = 8
            NT = NB // BL
            bh = sb("bh", [P, 2, FO], stack=st)
            fcs = sb("fcs", [P, 2, FO], stack=st)
            bfs = sb("bfs", [P, 2], stack=st)
            xr = sb("xr", [P, BL, D], stack=st)
            res = sb("res", [P, BL, D], stack=st)
            y = sb("y", [P, BL, FO], stack=st)
            z = sb("z", [P, BL, FO], stack=st)
            mask = sb("mask", [P, BL], stack=st)
            inv = sb("inv", [P, BL], stack=st)
            gate = sb("gate", [P, BL], stack=st)
            s_w, s_x, s_g, s_gs, s_out = sem("o_weights"), sem("o_x1"), sem("o_gate"), sem("o_sigmoid"), sem("o_stored")
            s_y, s_res, s_rows = sem("o_chain"), sem("o_added"), sem("o_rows")
            x1_v = x1_dr.rearrange("(b p) f -> p b f", p=P)
            out_v = out.rearrange("(b p) f -> p b f", p=P)
            block = st.enter_context(nc.Block())
            LINKS = 9

            @block.sync
            def _(sp):
                sp.dma_start(bh[:, :, :].rearrange("p a b -> p (a b)"), b_hop.partition_broadcast(P)).then_inc(s_w, 16)
                sp.dma_start(fcs[:, :, :].rearrange("p a b -> p (a b)"), fc.partition_broadcast(P)).then_inc(s_w, 16)
                sp.dma_start(bfs[:, :], bf.partition_broadcast(P)).then_inc(s_w, 16)

                def tiles(i):
                    wait(sp, s_res, i * 2)
                    sp.dma_start(xr[:, :, :], x1_v[:, bass.ds(i * BL, BL), :]).then_inc(s_x, 16)
                    sp.wait_ge(s_res, i * 2 + 2)
                    sp.dma_start(out_v[:, bass.ds(i * BL, BL), :], res[:, :, :]).then_inc(s_out, 16)
                looped(sp, NT, tiles)
                sp.wait_ge(s_out, NT * 16)

            @block.vector
            def _(v):
                v.wait_ge(s_w, 48)

                def tiles(i):
                    v.wait_ge(s_x, i * 16 + 16)
                    for hop in range(2):
                        n = i * 2 + hop
                        done = [0]

                        def link(ins):
                            done[0] += 1
                            ins.then_inc(s_y, 1)
                            v.wait_ge(s_y, n * LINKS + done[0])

                        big, deg_at = (big_a, 2 * FO) if hop == 0 else (big_b, FO)
                        deg = big[:, bass.ds(i * BL, BL), deg_at:deg_at + 1].rearrange("p b o -> p (b o)")
                        agg = big[:, bass.ds(i * BL, BL), 0:FO]
                        link(v.tensor_single_scalar(mask[:, :], deg, 0.0, op=ALU.is_gt))
                        link(v.tensor_tensor(inv[:, :], deg, mask[:, :], ALU.mult))
                        link(v.scalar_tensor_tensor(out=inv[:, :], in0=inv[:, :], scalar=1.0, in1=mask[:, :], op0=ALU.add, op1=ALU.subtract))
                        link(v.reciprocal(inv[:, :], inv[:, :]))
                        link(v.tensor_tensor(inv[:, :], inv[:, :], mask[:, :], ALU.mult))
                        link(v.tensor_tensor(y[:, :, :], agg, inv[:, :].unsqueeze(2).to_broadcast([P, BL, FO]), ALU.mult))
                        link(v.tensor_tensor(y[:, :, :], y[:, :, :], bh[:, hop, :].unsqueeze(1).to_broadcast([P, BL, FO]), ALU.add))
                        link(v.tensor_tensor(z[:, :, :], y[:, :, :], fcs[:, hop, :].unsqueeze(1).to_broadcast([P, BL, FO]), ALU.mult))
                        v.tensor_reduce(gate[:, :], z[:, :, :], AX.X, ALU.add).then_inc(s_g, 1)
                        v.wait_ge(s_gs, n + 1)
                        link(v.scalar_tensor_tensor(out=z[:, :, :], in0=y[:, :, :], scalar=0.0, in1=gate[:, :].unsqueeze(2).to_broadcast([P, BL, FO]),
                                                    op0=ALU.min, op1=ALU.mult))
                        v.scalar_tensor_tensor(out=z[:, :, :], in0=y[:, :, :], scalar=0.0, in1=z[:, :, :],
                                               op0=ALU.max, op1=ALU.add).then_inc(s_rows, 1)
                        v.wait_ge(s_rows, n + 1)
                        if hop == 0:
                            wait(v, s_out, i * 16)
                        v.tensor_tensor(res[:, :, hop * FO:(hop + 1) * FO], z[:, :, :], xr[:, :, hop * FO:(hop + 1) * FO],
                                        ALU.add).then_inc(s_res, 1)
                looped(v, NT, tiles)

            @block.scalar
            def _(act):
                act.wait_ge(s_w, 48)

                def tiles(i):
                    for hop in range(2):
                        act.wait_ge(s_g, i * 2 + hop + 1)
                        act.activation(gate[:, :], gate[:, :], ACT.Sigmoid, bias=bfs[:, hop:hop + 1]).then_inc(s_gs, 1)
                looped(act, NT, tiles)


def kernel(x, src, dst, edge_attr_16, edge_weight, L0_gnn_eW1, L0_gnn_eb1, L0_gnn_eW2, L0_gnn_eb2, L0_gnn_nW1,
           L0_gnn_nb1, L0_gnn_nW2, L0_gnn_nb2, L1_gnn_W0, L1_gnn_b0, L1_gnn_W1, L1_gnn_b1, L1_gnn_fc0, L1_gnn_bf0,
           L1_gnn_fc1, L1_gnn_bf1):
    import numpy as np
    import concourse.bacc as bacc
    from concourse import mybir as mb
    from concourse.bass_utils import run_bass_kernel_spmd as run

    x, src, dst, attr, weight = map(np.asarray, (x, src, dst, edge_attr_16, edge_weight))
    eW1, nW1 = np.asarray(L0_gnn_eW1), np.asarray(L0_gnn_nW1)
    n, e = x.shape[0], src.shape[0]
    blocks, cols = sizes(n, e)
    x_pad = np.zeros((blocks * P, D), np.float32)
    x_pad[:n] = x
    src_pad = np.full(P * cols, blocks * P - 1, np.int32)
    src_pad[:e] = src
    edges = np.zeros((P * cols, IN_WORDS), np.float32)
    edges[:e, :DE] = attr
    edges[:e, W_IN] = weight
    edges.view(np.int32)[:e, DST_IN] = dst
    row = lambda *parts: np.concatenate([np.asarray(p).reshape(-1) for p in parts])
    ins = {
        "x": x_pad, "src": src_pad.reshape(P, cols), "edges": edges,
        "w_node": np.concatenate([eW1[:D], eW1[D:2 * D], nW1[:D]], axis=1),
        "b_node": row(L0_gnn_eb1, np.zeros(D, np.float32), L0_gnn_nb1),
        "w_edge": np.tile(eW1[2 * D:], (P // DE, 1)), "e_w2": np.asarray(L0_gnn_eW2),
        "e_b2": row(L0_gnn_eb2),
        "w_update": np.concatenate([nW1[D:], np.asarray(L0_gnn_nW2), np.asarray(L1_gnn_W0), np.asarray(L1_gnn_W1)], axis=1),
        "n_b2": row(L0_gnn_nb2), "b_hop": row(L1_gnn_b0, L1_gnn_b1), "fc": row(L1_gnn_fc0, L1_gnn_fc1),
        "bf": row(L1_gnn_bf0, L1_gnn_bf1),
    }
    ins = {k: np.ascontiguousarray(v) for k, v in ins.items()}
    nc = bacc.Bacc("TRN2", target_bir_lowering=False, num_devices=1)
    args = [nc.dram_tensor("in_" + k, v.shape, mb.dt.from_np(v.dtype), kind="ExternalInput").ap() for k, v in ins.items()]
    out = nc.dram_tensor("out", (blocks * P, D), mb.dt.float32, kind="ExternalOutput").ap()
    gnn(nc, *args, out)
    r = run(nc, [{"in_" + k: v for k, v in ins.items()}], core_ids=[0])
    return r.results[0]["out"][:n]
```

```python
from contextlib import ExitStack

import concourse.bass as bass
from concourse import mybir

P = 128
D = 128
DE = 16
FO = 64
IN_WORDS = 20
W_IN, DST_IN = 16, 17
WORDS = 32
PART_WORDS = 3 * DE // 2
W_AT, LO_AT, DST_AT = 24, 25, 26
STACK = P
CH = 4
RING = 4
FILL = 64
COLS = 16
EPS = 1e-5


def up(a, b):
    return (a + b - 1) // b * b


def wait(eng, s, value):
    if not isinstance(value, int) or value > 0:
        eng.wait_ge(s, value)


def looped(eng, steps, body):
    body(0)
    with eng.Fori(1, steps) as i:
        body(i)


def looped_to_last(eng, steps, body):
    body(0)
    with eng.Fori(1, steps - 1) as i:
        body(i)
    body(steps - 1)


def sizes(n_nodes, n_edges):
    return up(n_nodes + P, 8 * P) // P, up(up(n_edges, P) // P, 2 * COLS)


def gnn(nc, n_nodes, n_edges, x, src, edges, w_node, b_node, w_edge, e_w2, e_b2, w_update, n_b2, b_hop, fc, bf, out):
    f32, bf16, i32 = mybir.dt.float32, mybir.dt.bfloat16, mybir.dt.int32
    ALU, ACT, AX = mybir.AluOpType, mybir.ActivationFunctionType, mybir.AxisListType
    NB = x.shape[0] // P
    C = src.shape[1]
    TILES = up((n_edges + up(n_nodes, P) // P * (P - 1)) // P, RING * CH)
    SLOTS = up(TILES * P + P * C - n_edges, P * FILL)
    GC = up(TILES, P) // P
    CHUNKS = TILES // CH
    NQ = NB // 4
    STEPS = C // COLS
    HCOLS = 4 * COLS
    HC = up(C, 2 * HCOLS)
    HW = NB // 4 * COLS
    assert HW <= 512 and NB <= P and NB % 8 == 0 and C % (2 * COLS) == 0 and CHUNKS % RING == 0 and NB < STEPS

    recs = nc.dram_tensor("recs", [SLOTS, WORDS], f32).ap()
    dst_tab = nc.dram_tensor("dst_tab", [NB * P, 3 * D], bf16).ap()
    node_dr = nc.dram_tensor("node_dr", [NB * P, 2 * D], f32).ap()
    blk_dr = nc.dram_tensor("blk_dr", [GC * P], i32).ap()
    hop_tab = nc.dram_tensor("hop_tab", [NB * P, 2 * FO], f32).ap()
    x1_dr = nc.dram_tensor("x1_dr", [NB * P, D], f32).ap()
    hop2_tab = nc.dram_tensor("hop2_tab", [NB * P, FO + 1], f32).ap()

    ctx = ExitStack()
    with ctx:
        def sb(name, shape, dt=f32, stack=ctx):
            return stack.enter_context(nc.sbuf_tensor(name, shape, dt))

        def sem(name):
            return ctx.enter_context(nc.semaphore(name))

        big_a = sb("big_a", [P, NB, 3 * D // 2])
        big_b = sb("big_b", [P, NB, D])
        src_tab = big_a[:, :, :].bitcast(bf16).rearrange("p b (s f) -> p b s f", s=3)
        ident = sb("ident", [P, P])
        iota_n = sb("iota_n", [P, P])
        eps = sb("eps", [P, 1])
        blk_row = sb("blk_row", [1, GC * P], i32)

        def tile_blocks(eng, first, n):
            _, blocks = nc.values_load_multi_w_load_instructions(
                blk_row[0:1, bass.ds(first, n)], engines=[eng.engine], min_val=0, max_val=NB - 1,
                skip_runtime_bounds_check_because="the table was clamped to the blocks' numbers")
            return list(blocks)

        with ExitStack() as st:
            spare = big_b[:, :, :].rearrange("p b f -> p (b f)")
            at = [0]

            def from_spare(words):
                at[0] += words
                assert at[0] <= NB * D
                return spare[:, at[0] - words:at[0]]

            src_i = from_spare(C).bitcast(i32)
            lo = from_spare(C)
            cmp_room = from_spare(max(GC * NB, HC))
            cmp = cmp_room[:, 0:GC * NB].rearrange("p (c b) -> p c b", b=NB)
            a_of = cmp_room[:, 0:HC // 2].bitcast(bf16)
            b_of = cmp_room[:, HC // 2:HC].bitcast(bf16)
            base = from_spare(NB * COLS).rearrange("p (b c) -> p b c", c=COLS)
            hi = sb("hi", [P, C], bf16, stack=st)
            iota_b = sb("iota_b", [P, NB, COLS], bf16, stack=st)
            iota_a = sb("iota_a", [P, 16, 8], bf16, stack=st)
            own = sb("own", [P, 16, 8], stack=st)
            ones = sb("ones", [P, P], bf16, stack=st)
            ones_f = sb("ones_f", [P, P], stack=st)
            below = sb("below", [P, P], bf16, stack=st)
            rest = sb("rest", [P, P], bf16, stack=st)
            zero = sb("zero", [P, 64], bf16, stack=st)
            hot = sb("hot", [P, 2, NB, COLS], bf16, stack=st)
            hot_a = sb("hot_a", [P, 2, HCOLS // 8, 16, 8], bf16, stack=st)
            hot_b = sb("hot_b8", [P, 2, HCOLS // 8, 8, 8], bf16, stack=st)
            prod = sb("prod", [P, NB, COLS], stack=st)
            tot = prod
            pos_f = sb("pos_f", [P, 2, COLS], stack=st)
            pos = sb("pos", [P, 2, COLS], i32, stack=st)
            edge = sb("edge", [P, 2, COLS, IN_WORDS], stack=st)
            rec = sb("rec", [P, 2, COLS, WORDS], stack=st)
            fill = sb("fill", [P, FILL, WORDS], stack=st)
            cnt = sb("cnt", [P, 4, NB], stack=st)
            cnt_i = sb("cnt_i", [P, NB], i32, stack=st)
            gval = sb("gval", [P, GC], stack=st)
            blk_f = sb("blk_f", [P, GC], stack=st)
            blk_i = sb("blk_i", [P, GC], i32, stack=st)
            wn = sb("wn", [P, 3 * D], stack=st)
            bn = sb("bn", [P, 3 * D], stack=st)
            xn = sb("xn", [P, 2, D], stack=st)
            h = sb("h", [P, 2, D], stack=st)
            hT = sb("hT", [P, 2, P], stack=st)
            tmp = sb("tmp", [P, 2, 2, D], stack=st)
            dst_st = sb("dst_st", [P, 2, 3, D], bf16, stack=st)
            node_st = sb("node_st", [P, 2, 2, D], stack=st)
            stats = sb("stats", [P, 2, 6], stack=st)
            mv = sb("mv", [P, 2, 2], stack=st)
            sd = sb("sd", [P, 2], stack=st)
            rstd = sb("rstd", [P, 2], stack=st)
            nmr = sb("nmr", [P, 2], stack=st)
            ps = st.enter_context(nc.psum_tensor("ps1", [P, 8, 512], f32))
            s_src, s_fill, s_fz, s_c, s_chain = sem("s_src"), sem("s_filled"), sem("s_fill_ready"), sem("s_consts"), sem("s_chain")
            s_hot, s_used, s_rank, s_prod = sem("s_hot"), sem("s_hot_counted"), sem("s_ranked"), sem("s_prod")
            s_pos, s_base, s_blk, s_blk_st = sem("s_pos"), sem("s_base"), sem("s_blk"), sem("s_blk_stored")
            s_edge = [sem("s_edge0"), sem("s_edge1")]
            s_sp, s_built = sem("s_split"), sem("s_built")
            s_sc = [sem("s_scattered0"), sem("s_scattered1")]
            s_placed, s_none = sem("s_counts_placed"), sem("s_none")
            s_turn, s_z, s_hot2 = sem("s_turn"), sem("s_z"), sem("s_hot2")
            s_red = sem("s_reduced")
            s_w, s_id, s_eps, s_x = sem("n_weights"), sem("n_ident"), sem("n_eps"), sem("n_x")
            s_st, s_mv, s_sd, s_rs, s_nm = sem("n_stats"), sem("n_mean_var"), sem("n_std"), sem("n_rstd"), sem("n_shift")
            s_h, s_tp, s_hT, s_mm = sem("n_h"), sem("n_hT_psum"), sem("n_hT"), sem("n_products")
            s_ev, s_nsp, s_nst, s_turn_v, s_turn_a = sem("n_evacuated"), sem("n_split"), sem("n_stored"), sem("n_turn_v"), sem("n_turn_a")
            e_v = edges.rearrange("(p c) w -> p c w", p=P)
            fill_v = recs.rearrange("(n p a) w -> n p (a w)", p=P, a=FILL)
            NF = fill_v.shape[0]
            x_v = x.rearrange("(b p) f -> p b f", p=P)
            tab_v = dst_tab.rearrange("(b p) f -> p b f", p=P)
            nod_v = node_dr.rearrange("(b p) f -> p b f", p=P)
            NP2 = NB // 2
            block = st.enter_context(nc.Block())

            def with_nodes(eng, step, node):
                def both(i):
                    step(i)
                    node(i)
                both(0)
                with eng.Fori(1, NP2) as i:
                    both(i)
                with eng.Fori(NP2, STEPS // 2) as i:
                    step(i)

            @block.sync
            def _(sp):
                sp.dma_start(src_i, src).then_inc(s_src, 16)
                sp.dma_start(wn[:, :], w_node).then_inc(s_w, 16)
                sp.dma_start(bn[:, :], b_node.partition_broadcast(P)).then_inc(s_w, 16)
                sp.wait_ge(s_fz, 1)
                with sp.Fori(0, NF) as i:
                    sp.dma_start(fill_v[bass.ds(i, 1), :, :].rearrange("a p w -> (a p) w"),
                                 fill[:, :, :].rearrange("p a w -> p (a w)")).then_inc(s_fill, 16)

                def load(i):
                    for u in range(2):
                        wait(sp, s_built, (i * 2 + u - 1) * 4)
                        sp.dma_start(edge[:, u, :, :], e_v[:, bass.ds((i * 2 + u) * COLS, COLS), :]).then_inc(s_edge[u], 16)
                looped(sp, STEPS // 2, load)
                sp.wait_ge(s_blk, 1)
                sp.dma_start(blk_dr.rearrange("(p c) -> p c", p=P), blk_i[:, :]).then_inc(s_blk_st, 16)
                sp.wait_ge(s_blk_st, 16)
                sp.dma_start(blk_row[:, :], blk_dr.unsqueeze(0)).then_inc(s_blk_st, 16)
                sp.wait_ge(s_blk_st, 32)
                for u in range(2):
                    sp.wait_ge(s_sc[u], STEPS // 2 * 16 * COLS)

            @block.gpsimd
            def _(pool):
                pool.memset(fill[:, :, :], 0.0).then_inc(s_z, 1)
                pool.memset(ident[:, :], 0.0).then_inc(s_z, 1)
                pool.memset(rec[:, :, :, :], 0.0).then_inc(s_z, 1)
                pool.memset(ones[:, :], 1.0).then_inc(s_z, 1)
                pool.memset(ones_f[:, :], 1.0).then_inc(s_z, 1)
                pool.wait_ge(s_z, 5)
                pool.memset(fill[:, :, LO_AT:LO_AT + 1], -1.0).then_inc(s_fz, 1)
                pool.affine_select(out=below[:, :], in_=ones[:, :], compare_op=ALU.is_gt, fill=0.0,
                                   base=0, pattern=[[1, P]], channel_multiplier=-1).then_inc(s_c, 1)
                pool.affine_select(out=rest[:, :], in_=ones[:, :], compare_op=ALU.is_ge, fill=0.0,
                                   base=0, pattern=[[-1, P]], channel_multiplier=1).then_inc(s_c, 1)
                pool.affine_select(out=ident[:, :], in_=ident[:, :], compare_op=ALU.not_equal, fill=1.0,
                                   base=0, pattern=[[-1, P]], channel_multiplier=1).then_inc(s_c, 1)
                pool.iota(iota_b[:, :, :], [[1, NB], [0, COLS]], 0, 0, allow_small_or_imprecise_dtypes=True).then_inc(s_c, 1)
                pool.iota(iota_a[:, :, :], [[1, 16], [0, 8]], 0, 0, allow_small_or_imprecise_dtypes=True).then_inc(s_c, 1)
                pool.iota(own[:, :, :], [[8, 16], [1, 8]], 0, -1, allow_small_or_imprecise_dtypes=True).then_inc(s_c, 1)
                pool.iota(iota_n[:, :], [[1, P]], 0, 0, allow_small_or_imprecise_dtypes=True).then_inc(s_c, 1)
                pool.iota(gval[:, :], [[P, GC]], 0, P * GC, allow_small_or_imprecise_dtypes=True).then_inc(s_c, 1)
                pool.wait_ge(s_fill, NF * 16)
                with pool.Fori(0, STEPS // 2) as i:
                    for u in range(2):
                        pool.wait_ge(s_pos, i * 2 + u + 1)
                        pool.sem_inc(s_turn, 1)
                        pool.wait_ge(s_built, (i * 2 + u) * 4 + 4)
                        pool.sem_inc(s_turn, 1)
                        for j in range(COLS):
                            pool.indirect_dma_start(recs, bass.IndirectOffsetOnAxis(ap=pos[:, u, j:j + 1], axis=0),
                                                    rec[:, u, j, :], None).then_inc(s_sc[u], 16)

            @block.vector
            def _(v):
                chain = [0]

                def link(ins):
                    chain[0] += 1
                    ins.then_inc(s_chain, 1)
                    v.wait_ge(s_chain, chain[0])

                v.memset(zero[:, :], 0.0).then_inc(s_id, 1)
                v.memset(eps[:, :], EPS).then_inc(s_eps, 1)
                v.memset(cmp_room[:, :].bitcast(bf16), -1.0).then_inc(s_none, 1)
                v.wait_ge(s_none, 1)
                v.wait_ge(s_src, 16)
                link(v.tensor_scalar(lo.bitcast(i32), src_i, 7, 7, op0=ALU.logical_shift_right, op1=ALU.bitwise_and))
                link(v.tensor_copy(b_of[:, 0:C], lo.bitcast(i32)))
                link(v.tensor_single_scalar(lo.bitcast(i32), src_i, 10, op=ALU.logical_shift_right))
                link(v.tensor_copy(a_of[:, 0:C], lo.bitcast(i32)))
                link(v.tensor_single_scalar(lo.bitcast(i32), src_i, 7, op=ALU.logical_shift_right))
                link(v.tensor_copy(hi[:, :], lo.bitcast(i32)))
                link(v.tensor_single_scalar(src_i, src_i, P - 1, op=ALU.bitwise_and))
                link(v.tensor_copy(lo, src_i))
                v.wait_ge(s_c, 8)
                link(v.tensor_single_scalar(own[:, :, :], own[:, :, :], 0.0, op=ALU.is_equal))

                def one_hot(n, u):
                    return v.tensor_tensor(hot[:, u, :, :], hi[:, bass.ds(n * COLS, COLS)].unsqueeze(1).to_broadcast([P, NB, COLS]),
                                           iota_b[:, :, :], ALU.is_equal)

                def digit(into, of, size, n):
                    of_step = of[:, bass.ds(n * HCOLS, HCOLS)].rearrange("p (g j) -> p g j", j=8)
                    return v.tensor_tensor(into, of_step.unsqueeze(2).to_broadcast([P, HCOLS // 8, size, 8]),
                                           iota_a[:, 0:size, :].unsqueeze(1).to_broadcast([P, HCOLS // 8, size, 8]), ALU.is_equal)

                with v.Fori(0, HC // HCOLS // 2) as i:
                    for u in range(2):
                        n = i * 2 + u
                        v.wait_ge(s_used, n + 1)
                        digit(hot_a[:, u, :, :, :], a_of, 16, n).then_inc(s_hot, 1)
                        digit(hot_b[:, u, :, :, :], b_of, 8, n).then_inc(s_hot, 1)
                v.wait_ge(s_used, HC // HCOLS + 2)
                for g in range(2):
                    v.tensor_tensor(base[:, :, 8 * g:8 * g + 8].rearrange("p (a b) j -> p a b j", b=8),
                                    ps[:, 4 + g, 0:64].rearrange("p (b j) -> p b j", b=8).unsqueeze(1).to_broadcast([P, NB // 8, 8, 8]),
                                    own[:, 0:NB // 8, :].unsqueeze(2).to_broadcast([P, NB // 8, 8, 8]), ALU.mult).then_inc(s_placed, 1)
                v.wait_ge(s_used, HC // HCOLS + 3)
                link(v.tensor_copy(tot[:, :, :].rearrange("p (g b) c -> p g (b c)", g=4), ps[:, 0:4, 0:HW]))
                link(v.tensor_reduce(cnt[:, 0, :], tot[:, :, :], AX.X, ALU.add))
                link(v.tensor_scalar(cnt[:, 1, :], cnt[:, 0, :], float(P - 1), None, ALU.add))
                link(v.tensor_copy(cnt_i[:, :], cnt[:, 1, :]))
                link(v.tensor_single_scalar(cnt_i[:, :], cnt_i[:, :], 7, op=ALU.logical_shift_right))
                link(v.tensor_single_scalar(cnt_i[:, :], cnt_i[:, :], 7, op=ALU.logical_shift_left))
                link(v.tensor_copy(cnt[:, 1, :], cnt_i[:, :]))
                link(v.memset(cnt[:, 2, :], 1.0))
                link(v.tensor_tensor_scan(cnt[:, 3, :], cnt[:, 2, :], cnt[:, 1, :], 0.0, ALU.mult, ALU.add))
                link(v.tensor_tensor(base[:, :, 0], cnt[:, 3, :], cnt[:, 1, :], ALU.subtract))
                for j in range(1, COLS):
                    link(v.tensor_tensor(base[:, :, j], base[:, :, j - 1], tot[:, :, j - 1], ALU.add))
                v.memset(hot[:, 1, :, :], 0.0).then_inc(s_base, 1)
                link(v.tensor_tensor(cmp, cnt[:, 3, :].unsqueeze(1).to_broadcast([P, GC, NB]),
                                     gval[:, :].unsqueeze(2).to_broadcast([P, GC, NB]), ALU.is_le))
                link(v.tensor_reduce(blk_f[:, :], cmp, AX.X, ALU.add))
                link(v.tensor_scalar(blk_f[:, :], blk_f[:, :], float(NB - 1), None, ALU.min))
                v.tensor_copy(blk_i[:, :], blk_f[:, :]).then_inc(s_blk, 1)

                def rank(i):
                    for u in range(2):
                        n = i * 2 + u
                        one_hot(n, u).then_inc(s_hot2, 1)
                        v.wait_ge(s_edge[u], i * 16 + 16)
                        wait(v, s_sc[u], i * (16 * COLS))
                        parts = rec[:, u, :, 0:PART_WORDS].bitcast(bf16).rearrange("p c (s f) -> p c s f", s=3)
                        rem = edge[:, u, :, 0:DE]
                        for s in range(3):
                            v.tensor_copy(parts[:, :, s, :], rem).then_inc(s_sp if s < 2 else s_built, 1)
                            if s < 2:
                                v.wait_ge(s_sp, n * 4 + 2 * s + 1)
                                v.tensor_tensor(rem, rem, parts[:, :, s, :], ALU.subtract).then_inc(s_sp, 1)
                                v.wait_ge(s_sp, n * 4 + 2 * s + 2)
                        v.tensor_copy(rec[:, u, :, W_AT:W_AT + 1], edge[:, u, :, W_IN:W_IN + 1]).then_inc(s_built, 1)
                        v.tensor_copy(rec[:, u, :, DST_AT:DST_AT + 1].bitcast(i32), edge[:, u, :, DST_IN:DST_IN + 1].bitcast(i32)).then_inc(s_built, 1)
                        v.tensor_copy(rec[:, u, :, LO_AT:LO_AT + 1], lo[:, bass.ds(n * COLS, COLS)].unsqueeze(2)).then_inc(s_built, 1)
                        v.wait_ge(s_rank, n + 1)
                        v.tensor_tensor(prod[:, :, :].rearrange("p (g b) c -> p g (b c)", g=4), hot[:, u, :, :].rearrange("p (g b) c -> p g (b c)", g=4),
                                        ps[:, 0:4, 0:HW], ALU.mult).then_inc(s_prod, 1)
                        v.wait_ge(s_prod, n + 1)
                        v.tensor_reduce(pos_f[:, u, :], prod[:, :, :].rearrange("p b c -> p c b"), AX.X, ALU.add).then_inc(s_red, 1)
                        v.wait_ge(s_red, n + 1)
                        v.tensor_copy(pos[:, u, :], pos_f[:, u, :]).then_inc(s_pos, 1)

                def node(i):
                    v.wait_ge(s_x, i * 16 + 16)
                    for t in range(2):
                        v.bn_stats(stats[:, t, :], xn[:, t, :]).then_inc(s_st, 1)
                    v.wait_ge(s_st, i * 2 + 2)
                    v.sem_inc(s_turn_v, 1)
                    for t in range(2):
                        v.bn_aggr(mv[:, t, :], stats[:, t, :]).then_inc(s_mv, 1)
                    v.wait_ge(s_sd, i + 1)
                    v.reciprocal(rstd[:, :], sd[:, :]).then_inc(s_rs, 1)
                    v.wait_ge(s_rs, i + 1)
                    v.scalar_tensor_tensor(out=nmr[:, :], in0=mv[:, :, 0], scalar=-1.0, in1=rstd[:, :],
                                           op0=ALU.mult, op1=ALU.mult).then_inc(s_nm, 1)
                    wait(v, s_nst, i * 32)
                    v.wait_ge(s_h, i * 2 + 2)
                    v.tensor_tensor(node_st[:, :, 1, :], xn[:, :, :], h[:, :, :], ALU.add).then_inc(s_ev, 1)
                    v.wait_ge(s_mm, i + 1)
                    v.tensor_tensor(tmp[:, :, :, :].rearrange("p t s f -> p t (s f)"), ps[:, 5:7, 0:2 * D],
                                    bn[:, 0:2 * D].unsqueeze(1).to_broadcast([P, 2, 2 * D]), ALU.add).then_inc(s_ev, 1)
                    v.tensor_tensor(node_st[:, :, 0, :], ps[:, 5:7, 2 * D:3 * D],
                                    bn[:, 2 * D:3 * D].unsqueeze(1).to_broadcast([P, 2, D]), ALU.add).then_inc(s_ev, 1)
                    v.wait_ge(s_ev, i * 3 + 2)
                    for s in range(3):
                        for side, part in enumerate((src_tab[:, bass.ds(i * 2, 2), s, :], dst_st[:, :, s, :])):
                            v.tensor_copy(part, tmp[:, :, side, :]).then_inc(s_nsp, 1)
                        v.wait_ge(s_nsp, i * 10 + 4 * s + 2)
                        if s < 2:
                            for side, part in enumerate((src_tab[:, bass.ds(i * 2, 2), s, :], dst_st[:, :, s, :])):
                                v.tensor_tensor(tmp[:, :, side, :], tmp[:, :, side, :], part, ALU.subtract).then_inc(s_nsp, 1)
                            v.wait_ge(s_nsp, i * 10 + 4 * s + 4)
                with_nodes(v, rank, node)

            @block.scalar
            def _(act):
                act.wait_ge(s_eps, 1)

                def node(i):
                    wait(act, s_ev, i * 3)
                    act.dma_start(xn[:, :, :], x_v[:, bass.ds(i * 2, 2), :]).then_inc(s_x, 16)
                    act.wait_ge(s_mv, i * 2 + 2)
                    act.activation(sd[:, :], mv[:, :, 1], ACT.Sqrt, bias=eps[:, :]).then_inc(s_sd, 1)
                    act.wait_ge(s_nm, i + 1)
                    for t in range(2):
                        act.activation(h[:, t, :], xn[:, t, :], ACT.Relu, bias=nmr[:, t:t + 1], scale=rstd[:, t:t + 1]).then_inc(s_h, 1)
                    act.wait_ge(s_tp, i + 1)
                    act.activation(hT[:, :, :].rearrange("p a b -> p (a b)"), ps[:, 4, 0:2 * P], ACT.Copy).then_inc(s_hT, 1)
                    act.wait_ge(s_nsp, i * 10 + 10)
                    act.sem_inc(s_turn_a, 1)
                    act.wait_ge(s_ev, i * 3 + 3)
                    act.dma_start(tab_v[:, bass.ds(i * 2, 2), :], dst_st[:, :, :, :].rearrange("p t s f -> p t (s f)")).then_inc(s_nst, 16)
                    act.dma_start(nod_v[:, bass.ds(i * 2, 2), :], node_st[:, :, :, :].rearrange("p t s f -> p t (s f)")).then_inc(s_nst, 16)
                looped(act, NP2, node)
                act.wait_ge(s_nst, NP2 * 32)

            @block.tensor
            def _(pe):
                pe.wait_ge(s_c, 8)
                pe.wait_ge(s_id, 1)

                def quarter(u, g):
                    return hot[:, u, g * NB // 4:(g + 1) * NB // 4, :].rearrange("p b c -> p (b c)")

                for g in range(2):
                    last = pe.matmul(ps[:, 4 + g, 0:64], ones[:, :], zero[:, 0:64], start=True, stop=False, skip_group_check=True)
                last.then_inc(s_used, 2)
                with pe.Fori(0, HC // HCOLS // 2) as i:
                    for u in range(2):
                        pe.wait_ge(s_hot, (i * 2 + u) * 2 + 2)
                        for g in range(HCOLS // 8):
                            last = pe.matmul(ps[:, 4 + g % 2, 0:64], hot_a[:, u, g, :, :].rearrange("p a j -> p (a j)"),
                                             hot_b[:, u, g, :, :].rearrange("p b j -> p (b j)"), start=False, stop=False, skip_group_check=True)
                        last.then_inc(s_used, 1)
                pe.wait_ge(s_placed, 2)
                for g in range(4):
                    last = pe.matmul(ps[:, g, 0:HW], ones_f[:, :], base[:, g * NB // 4:(g + 1) * NB // 4, :].rearrange("p b c -> p (b c)"),
                                     start=True, stop=True)
                last.then_inc(s_used, 1)
                pe.wait_ge(s_base, 1)
                for g in range(4):
                    pe.matmul(ps[:, g, 0:HW], ident[:, :], base[:, g * NB // 4:(g + 1) * NB // 4, :].rearrange("p b c -> p (b c)"),
                              start=True, stop=False, skip_group_check=True)
                pe.wait_ge(s_w, 32)

                def rank(i):
                    for u in range(2):
                        n = i * 2 + u
                        pe.wait_ge(s_hot2, n + 1)
                        wait(pe, s_prod, n)
                        for g in range(4):
                            pe.matmul(ps[:, g, 0:HW], rest[:, :], quarter(1 - u, g), start=False, stop=False, skip_group_check=True)
                            last = pe.matmul(ps[:, g, 0:HW], below[:, :], quarter(u, g), start=False, stop=False, skip_group_check=True)
                        last.then_inc(s_rank, 1)

                def node(i):
                    pe.wait_ge(s_h, i * 2 + 2)
                    for t in range(2):
                        last = pe.transpose(ps[:, 4, t * P:(t + 1) * P], h[:, t, :], ident[:, :])
                    last.then_inc(s_tp, 1)
                    pe.wait_ge(s_hT, i + 1)
                    wait(pe, s_ev, i * 3)
                    for t in range(2):
                        last = pe.matmul(ps[:, 5 + t, 0:3 * D], hT[:, t, :], wn[:, :], start=True, stop=True)
                    last.then_inc(s_mm, 1)
                with_nodes(pe, rank, node)

        with ExitStack() as st:
            w_f = sb("w_f", [P, 2, D], stack=st)
            w_part = sb("w_part", [P, 3, 2, D], bf16, stack=st)
            we = sb("we", [P, D], bf16, stack=st)
            w2 = sb("w2", [P, D], stack=st)
            b2 = sb("b2", [P, CH, D], bf16, stack=st)
            ones = sb("ones_l0", [P, P], bf16, stack=st)
            ident_b = sb("ident_b", [P, P], bf16, stack=st)
            rec = sb("rec_l0", [P, RING, CH, WORDS], stack=st)
            gat = sb("gat_l0", [P, RING, CH, 3, D], bf16, stack=st)
            dup = sb("dup", [P, 2, CH, STACK], bf16, stack=st)
            hot = sb("hot_l0", [P, RING, CH, P], stack=st)
            hot_b = sb("hot_b", [P, 2, CH, P], bf16, stack=st)
            turned = sb("turned", [P, 2, 2, CH * P], bf16, stack=st)
            hid = sb("hid", [P, 2, CH * P], stack=st)
            msg = sb("msg", [P, 2, CH * D], stack=st)
            ps = st.enter_context(nc.psum_tensor("ps2", [P, 8, 512], f32))
            turned_ps = [ps[:, c, :].bitcast(bf16).rearrange("p (s e) -> p s e", s=2) for c in range(2)]
            PRE1, PRE2, SUMS = 2, 3, 4
            s_w, s_zero, s_wp = sem("e_weights"), sem("e_zeroed"), sem("e_weight_parts")
            s_rec = [sem(f"e_rec{r}") for r in range(RING)]
            s_gat = [sem(f"e_gathered{r}") for r in range(RING)]
            s_hot, s_tp, s_cp, s_z = sem("e_hot"), sem("e_transposed"), sem("e_copied"), sem("e_pre1")
            s_hid, s_mp, s_m, s_ag, s_add = sem("e_hid"), sem("e_pre2"), sem("e_msg"), sem("e_tile_sums"), sem("e_added")
            s_turn, s_load_turn = sem("e_turn"), sem("e_load_turn")
            rec_v = recs.rearrange("(k t p) w -> k p t w", t=CH, p=P)
            ZEROED = 4 + 6 + 1
            HOTS = 5
            block = st.enter_context(nc.Block())

            @block.sync
            def _(sp):
                sp.dma_start(w_f[:, 0, :], w_edge).then_inc(s_w, 16)
                sp.dma_start(w_f[:, 1, :], e_b2.partition_broadcast(P)).then_inc(s_w, 16)
                sp.dma_start(w2[:, :], e_w2).then_inc(s_w, 16)

                def load(i, r):
                    k = i * RING + r
                    wait(sp, s_tp, k - RING + 1)
                    sp.sem_inc(s_load_turn, 1)
                    wait(sp, s_gat[r], i * (16 * CH))
                    sp.dma_start(rec[:, r, :, :], rec_v[bass.ds(k, 1), :, :, :].rearrange("k p t w -> (k p) t w")).then_inc(s_rec[r], 16)
                looped(sp, CHUNKS // RING, lambda i: [load(i, r) for r in range(RING)])

            @block.gpsimd
            def _(pool):
                def gather(i, r):
                    k = i * RING + r
                    pool.wait_ge(s_rec[r], i * 16 + 16)
                    pool.sem_inc(s_turn, 1)
                    if not isinstance(i, int) or i > 0:
                        pool.wait_ge(s_z, k - RING + 1)
                        pool.sem_inc(s_turn, 1)
                    for t in range(CH):
                        pool.indirect_dma_start(gat[:, r, t, :, :].rearrange("p s f -> p (s f)"), None, dst_tab,
                                                bass.IndirectOffsetOnAxis(ap=rec[:, r, t, DST_AT:DST_AT + 1].bitcast(i32), axis=0)).then_inc(s_gat[r], 16)
                looped(pool, CHUNKS // RING, lambda i: [gather(i, r) for r in range(RING)])

            @block.vector
            def _(v):
                zeroed = [0]

                def begun(ins):
                    zeroed[0] += 1
                    ins.then_inc(s_zero, 1)

                begun(v.memset(dup[:, :, :, :], 0.0))
                begun(v.memset(b2[:, :, :], 0.0))
                begun(v.memset(ones[:, :], 1.0))
                begun(v.tensor_copy(ident_b[:, :], ident[:, :]))
                v.wait_ge(s_zero, 4)

                def one_hot(k, i, r):
                    v.wait_ge(s_rec[r], i * 16 + 16)
                    wait(v, s_ag, k - RING + 1)
                    v.tensor_tensor(hot[:, r, :, :], rec[:, r, :, LO_AT:LO_AT + 1].to_broadcast([P, CH, P]),
                                    iota_n[:, :].unsqueeze(1).to_broadcast([P, CH, P]), ALU.is_equal).then_inc(s_hot, 1)
                    wait(v, s_tp, k - 1)
                    parts = rec[:, r, :, 0:PART_WORDS].bitcast(bf16)
                    for at, n in ((0, 3), (4, 2), (6, 1)):
                        v.tensor_copy(dup[:, r % 2, :, at * DE:(at + n) * DE], parts[:, :, 0:n * DE]).then_inc(s_hot, 1)
                    v.wait_ge(s_hot, k * HOTS + 1)
                    v.tensor_copy(hot_b[:, r % 2, :, :], hot[:, r, :, :]).then_inc(s_hot, 1)

                def add(k, r, blocks):
                    v.wait_ge(s_ag, k + 1)
                    for t in range(CH):
                        into = big_b[:, bass.ds(blocks[t], 1), :].rearrange("p a f -> p (a f)")
                        wait(v, s_add, k * CH + t)
                        v.tensor_tensor(into, into, ps[:, SUMS + r % 2, t * D:(t + 1) * D], ALU.add).then_inc(s_add, 1)

                def chunk(i):
                    first, last = isinstance(i, int) and i == 0, isinstance(i, int) and i > 0
                    skip = CH if first else 0
                    blocks = [None] * skip + tile_blocks(v, i * (RING * CH) - CH + skip, RING * CH - skip)
                    for r in range(RING):
                        k = i * RING + r
                        if not (last and r >= RING - 2):
                            one_hot(k + 2, i + (r + 2) // RING, (r + 2) % RING)
                        if not (first and r == 0):
                            add(k - 1, (r - 1) % RING, blocks[r * CH:(r + 1) * CH])

                one_hot(0, 0, 0)
                v.wait_ge(s_w, 48)
                for s in range(3):
                    v.tensor_copy(w_part[:, s, :, :], w_f[:, :, :]).then_inc(s_wp, 1)
                    v.wait_ge(s_wp, 2 * s + 1)
                    v.tensor_tensor(w_f[:, :, :], w_f[:, :, :], w_part[:, s, :, :], ALU.subtract).then_inc(s_wp, 1)
                    v.wait_ge(s_wp, 2 * s + 2)
                for s, (a, b) in enumerate(((0, 64), (64, 96), (96, 128))):
                    begun(v.tensor_copy(we[a:b, :], w_part[a:b, s, 0, :]))
                    begun(v.tensor_copy(b2[32 * s:32 * s + 1, :, :], w_part[32 * s:32 * s + 1, s, 1:2, :].to_broadcast([1, CH, D])))
                begun(v.memset(big_b[:, :, :], 0.0))
                v.wait_ge(s_zero, ZEROED)
                one_hot(1, 0, 1)
                looped_to_last(v, CHUNKS // RING, chunk)
                add(CHUNKS - 1, RING - 1, tile_blocks(v, (CHUNKS - 1) * CH, CH))

            @block.scalar
            def _(act):
                def copies(k, r):
                    act.wait_ge(s_tp, k + 1)
                    act.activation(turned[:, r % 2, :, :], turned_ps[r % 2], ACT.Copy).then_inc(s_cp, 1)

                def silu_msg(k, r):
                    act.wait_ge(s_mp, k + 1)
                    wait(act, s_ag, k - 1)
                    act.activation(msg[:, r % 2, :], ps[:, PRE2, :], ACT.Silu).then_inc(s_m, 1)

                def silu_hid(k, r):
                    act.wait_ge(s_z, k + 1)
                    act.activation(hid[:, r % 2, :], ps[:, PRE1, :], ACT.Silu).then_inc(s_hid, 1)

                def chunk(i):
                    last = isinstance(i, int) and i > 0
                    for r in range(RING):
                        k = i * RING + r
                        if not (last and r == RING - 1):
                            copies(k + 1, (r + 1) % RING)
                        if not (isinstance(k, int) and k == 0):
                            silu_msg(k - 1, (r - 1) % RING)
                        silu_hid(k, r)
                copies(0, 0)
                looped_to_last(act, CHUNKS // RING, chunk)
                silu_msg(CHUNKS - 1, RING - 1)

            @block.tensor
            def _(pe):
                pe.wait_ge(s_w, 48)
                pe.wait_ge(s_zero, ZEROED)

                def transposes(k, r):
                    pe.wait_ge(s_hot, k * HOTS + HOTS)
                    for t in range(CH):
                        pe.transpose(turned_ps[r % 2][:, 0, t * P:(t + 1) * P], hot_b[:, r % 2, t, :], ident_b[:, :])
                    for t in range(CH):
                        last = pe.transpose(turned_ps[r % 2][:, 1, t * P:(t + 1) * P], dup[:, r % 2, t, :], ident_b[:, :])
                    last.then_inc(s_tp, 1)

                def pre1(k, i, r, blocks):
                    pe.wait_ge(s_cp, k + 1)
                    pe.matmul(ps[:, PRE1, :], we[:, :], turned[:, r % 2, 1, :], start=True, stop=False, skip_group_check=True)
                    pe.wait_ge(s_gat[r], i * (16 * CH) + 16 * CH)
                    for t in range(CH):
                        for s in range(3):
                            pe.matmul(ps[:, PRE1, t * P:(t + 1) * P], src_tab[:, bass.ds(blocks[t], 1), s, :].rearrange("p a f -> p (a f)"),
                                      turned[:, r % 2, 0, t * P:(t + 1) * P], start=False, stop=False, skip_group_check=True)
                            last = pe.matmul(ps[:, PRE1, t * P:(t + 1) * P], gat[:, r, t, s, :], ident_b[:, :],
                                             start=False, stop=(s == 2), skip_group_check=True)
                    last.then_inc(s_z, 1)

                def pre2(k, r):
                    pe.wait_ge(s_hid, k + 1)
                    pe.matmul(ps[:, PRE2, :], ones[:, :], b2[:, :, :].rearrange("p t f -> p (t f)"), start=True, stop=False, skip_group_check=True)
                    for t in range(CH):
                        last = pe.matmul(ps[:, PRE2, t * D:(t + 1) * D], hid[:, r % 2, t * P:(t + 1) * P], w2[:, :], start=False, stop=True,
                                         skip_group_check=True)
                    last.then_inc(s_mp, 1)

                def sums(k, r):
                    pe.wait_ge(s_m, k + 1)
                    wait(pe, s_add, (k - 1) * CH)
                    for t in range(CH):
                        last = pe.matmul(ps[:, SUMS + r % 2, t * D:(t + 1) * D], hot[:, r, t, :], msg[:, r % 2, t * D:(t + 1) * D],
                                         start=True, stop=True)
                    last.then_inc(s_ag, 1)

                def chunk(i):
                    last = isinstance(i, int) and i > 0
                    blocks = tile_blocks(pe, i * (RING * CH), RING * CH)
                    for r in range(RING):
                        k = i * RING + r
                        first = isinstance(k, int) and k == 0
                        if not (last and r == RING - 1):
                            transposes(k + 1, (r + 1) % RING)
                        if not first:
                            pre2(k - 1, (r - 1) % RING)
                        pre1(k, i, r, blocks[r * CH:(r + 1) * CH])
                        if not first:
                            sums(k - 1, (r - 1) % RING)
                transposes(0, 0)
                looped_to_last(pe, CHUNKS // RING, chunk)
                pre2(CHUNKS - 1, RING - 1)
                sums(CHUNKS - 1, RING - 1)

        with ExitStack() as st:
            wu = sb("wu", [P, 3 * D], stack=st)
            bu = sb("bu", [P, D], stack=st)
            nd = sb("nd", [P, 2, 4, 2 * D], stack=st)
            sums0 = sb("sums0", [P, 2, 4, D], stack=st)
            t1 = sb("t1", [P, 2, 4, P], stack=st)
            u1 = sb("u1", [P, 2, 4, D], stack=st)
            u2 = sb("u2", [P, 2, 4, D], stack=st)
            t2 = sb("t2", [P, 2, 4, P], stack=st)
            x1 = sb("x1", [P, 2, 4, D], stack=st)
            h2 = sb("h2", [P, 2, 4, D], stack=st)
            t3 = sb("t3", [P, 2, 4, P], stack=st)
            hop = sb("hop", [P, 2, 4, D], stack=st)
            stats = sb("stats2", [P, 2, 4, 6], stack=st)
            mv = sb("mv2", [P, 2, 4, 2], stack=st)
            sd = sb("sd2", [P, 2, 4], stack=st)
            rstd = sb("rstd2", [P, 2, 4], stack=st)
            nmr = sb("nmr2", [P, 2, 4], stack=st)
            ps = st.enter_context(nc.psum_tensor("ps3", [P, 8, 512], f32))
            s_w = sem("u_weights")
            s_nd = [sem("u_nodes0"), sem("u_nodes1")]
            s_pe, s_t, s_u1, s_u2 = sem("u_products"), sem("u_copied"), sem("u_part"), sem("u_silu")
            s_x1, s_st, s_mv, s_rs, s_nm, s_h2, s_hop = (sem("u_x1"), sem("u_stats"), sem("u_mean_var"), sem("u_rstd"),
                                                         sem("u_shift"), sem("u_h2"), sem("u_hop"))
            s_turn2, s_sd2, s_turn_v2 = sem('u_turn'), sem('u_std'), sem('u_turn_v')
            s_xa = sem("u_x1_part")
            s_out = [sem("u_stored0"), sem("u_stored1")]
            nod_v = node_dr.rearrange("(b p) f -> p b f", p=P)
            x1_v = x1_dr.rearrange("(b p) f -> p b f", p=P)
            hop_v = hop_tab.rearrange("(b p) f -> p b f", p=P)
            block = st.enter_context(nc.Block())

            @block.sync
            def _(sp):
                sp.dma_start(wu[:, :], w_update).then_inc(s_w, 16)
                sp.dma_start(bu[:, :], n_b2.partition_broadcast(P)).then_inc(s_w, 16)

                def quads(i):
                    for u in range(2):
                        wait(sp, s_x1, (i * 2 + u) - 1)
                        sp.dma_start(nd[:, u, :, :], nod_v[:, bass.ds(i * 8 + 4 * u, 4), :]).then_inc(s_nd[u], 16)
                looped(sp, NQ // 2, quads)

            @block.gpsimd
            def _(pool):
                def quads(i):
                    for u in range(2):
                        n = i * 2 + u
                        pool.wait_ge(s_x1, n + 1)
                        pool.sem_inc(s_turn2, 1)
                        pool.dma_start(x1_v[:, bass.ds(i * 8 + 4 * u, 4), :], x1[:, u, :, :]).then_inc(s_out[u], 16)
                        pool.wait_ge(s_hop, n + 1)
                        pool.sem_inc(s_turn2, 1)
                        pool.dma_start(hop_v[:, bass.ds(i * 8 + 4 * u, 4), :], hop[:, u, :, :]).then_inc(s_out[u], 16)
                looped(pool, NQ // 2, quads)
                for u in range(2):
                    pool.wait_ge(s_out[u], NQ // 2 * 32)

            def after(i, steps, step, u):
                return i * (2 * steps) + (2 * step + u + 1)

            def bank(u, b):
                return ps[:, 4 * u + b, :].rearrange("p (t f) -> p t f", t=4)

            @block.vector
            def _(v):
                v.wait_ge(s_w, 32)

                def pair(i):
                    for u in range(2):
                        v.wait_ge(s_nd[u], i * 16 + 16)
                        v.wait_ge(s_pe, after(i, 6, 1, u))
                        v.tensor_tensor(u1[:, u, :, :], bank(u, 1), nd[:, u, :, 0:D], ALU.add).then_inc(s_u1, 1)
                    for u in range(2):
                        v.wait_ge(s_pe, after(i, 6, 3, u))
                        wait(v, s_out[u], i * 32)
                        v.tensor_tensor(x1[:, u, :, :], bank(u, 3), nd[:, u, :, D:2 * D], ALU.add).then_inc(s_xa, 1)
                    for u in range(2):
                        n = i * 2 + u
                        v.wait_ge(s_xa, n + 1)
                        v.tensor_tensor(x1[:, u, :, :], x1[:, u, :, :], bu[:, :].unsqueeze(1).to_broadcast([P, 4, D]), ALU.add).then_inc(s_x1, 1)
                    for u in range(2):
                        n = i * 2 + u
                        v.wait_ge(s_x1, n + 1)
                        for t in range(4):
                            v.bn_stats(stats[:, u, t, :], x1[:, u, t, :]).then_inc(s_st, 1)
                    v.wait_ge(s_st, i * 8 + 8)
                    v.sem_inc(s_turn_v2, 1)
                    for u in range(2):
                        for t in range(4):
                            v.bn_aggr(mv[:, u, t, :], stats[:, u, t, :]).then_inc(s_mv, 1)
                    v.wait_ge(s_sd2, i + 1)
                    v.reciprocal(rstd[:, :, :], sd[:, :, :]).then_inc(s_rs, 1)
                    v.wait_ge(s_rs, i + 1)
                    v.scalar_tensor_tensor(out=nmr[:, :, :], in0=mv[:, :, :, 0], scalar=-1.0, in1=rstd[:, :, :],
                                           op0=ALU.mult, op1=ALU.mult).then_inc(s_nm, 1)
                    for u in range(2):
                        v.wait_ge(s_pe, after(i, 6, 5, u))
                        v.tensor_copy(hop[:, u, :, :], bank(u, 1)).then_inc(s_hop, 1)
                looped(v, NQ // 2, pair)

            @block.scalar
            def _(act):
                def copied(i, u, step, into, b):
                    act.wait_ge(s_pe, after(i, 6, step, u))
                    act.activation(into[:, u, :, :], bank(u, b), ACT.Copy).then_inc(s_t, 1)

                def pair(i):
                    for u in range(2):
                        act.activation(sums0[:, u, :, :], big_b[:, bass.ds(i * 8 + 4 * u, 4), :], ACT.Copy).then_inc(s_t, 1)
                    for u in range(2):
                        copied(i, u, 0, t1, 0)
                    for u in range(2):
                        n = i * 2 + u
                        act.wait_ge(s_u1, n + 1)
                        act.activation(u2[:, u, :, :], u1[:, u, :, :], ACT.Silu).then_inc(s_u2, 1)
                    for u in range(2):
                        copied(i, u, 2, t2, 2)
                    act.wait_ge(s_mv, i * 8 + 8)
                    act.activation(sd[:, :, :], mv[:, :, :, 1], ACT.Sqrt, bias=eps[:, :]).then_inc(s_sd2, 1)
                    act.wait_ge(s_nm, i + 1)
                    for u in range(2):
                        for t in range(4):
                            act.activation(h2[:, u, t, :], x1[:, u, t, :], ACT.Relu, bias=nmr[:, u, t:t + 1],
                                           scale=rstd[:, u, t:t + 1]).then_inc(s_h2, 1)
                    for u in range(2):
                        copied(i, u, 4, t3, 0)
                looped(act, NQ // 2, pair)

            @block.tensor
            def _(pe):
                pe.wait_ge(s_w, 32)

                def transposed(u, b, rows):
                    for t in range(4):
                        last = pe.transpose(bank(u, b)[:, t, :], rows[:, u, t, :], ident[:, :])
                    last.then_inc(s_pe, 1)

                def products(u, b, lhsT, w):
                    for t in range(4):
                        last = pe.matmul(bank(u, b)[:, t, :], lhsT[:, u, t, :], wu[:, w * D:(w + 1) * D], start=True, stop=True)
                    last.then_inc(s_pe, 1)

                def pair(i):
                    for u in range(2):
                        pe.wait_ge(s_t, after(i, 4, 0, u))
                        transposed(u, 0, sums0)
                    for u in range(2):
                        n = i * 2 + u
                        pe.wait_ge(s_t, after(i, 4, 1, u))
                        wait(pe, s_hop, n - 1)
                        products(u, 1, t1, 0)
                    for u in range(2):
                        n = i * 2 + u
                        pe.wait_ge(s_u2, n + 1)
                        transposed(u, 2, u2)
                    for u in range(2):
                        pe.wait_ge(s_t, after(i, 4, 2, u))
                        products(u, 3, t2, 1)
                    for u in range(2):
                        pe.wait_ge(s_h2, i * 8 + 4 * u + 4)
                        transposed(u, 0, h2)
                    for u in range(2):
                        pe.wait_ge(s_t, after(i, 4, 3, u))
                        products(u, 1, t3, 2)
                looped(pe, NQ // 2, pair)

        def hop_pass(name, table, width, ones_at, into_tile):
            cols = into_tile.shape[2]
            with ExitStack() as st:
                rec = sb(name + "_rec", [P, RING, CH, WORDS], stack=st)
                gat = sb(name + "_gat", [P, RING, CH, 2 * FO + 4], stack=st)
                hot = sb(name + "_hot", [P, RING, CH, P], stack=st)
                ps = st.enter_context(nc.psum_tensor(name + "_ps", [P, 8, 512], f32))
                s_rec = [sem(f"{name}_recs{r}") for r in range(RING)]
                s_gat = [sem(f"{name}_gathered{r}") for r in range(RING)]
                s_hot, s_ag, s_add, s_zero, s_turn = (sem(name + "_hots"), sem(name + "_group_sums"), sem(name + "_added"),
                                                      sem(name + "_zeroed"), sem(name + "_turn"))
                s_load_turn = sem(name + "_load_turn")
                rec_v = recs.rearrange("(k t p) w -> k p t w", t=CH, p=P)

                def bank(r, t):
                    return ps[:, 2 * r + t // 2, t % 2 * 256:t % 2 * 256 + cols]

                block = st.enter_context(nc.Block())

                @block.sync
                def _(sp):
                    def load(i, r):
                        k = i * RING + r
                        wait(sp, s_hot, (k - RING + 1) * CH)
                        sp.sem_inc(s_load_turn, 1)
                        wait(sp, s_gat[r], i * (16 * CH))
                        sp.dma_start(rec[:, r, :, :], rec_v[bass.ds(k, 1), :, :, :].rearrange("k p t w -> (k p) t w")).then_inc(s_rec[r], 16)
                    looped(sp, CHUNKS // RING, lambda i: [load(i, r) for r in range(RING)])

                @block.gpsimd
                def _(pool):
                    if ones_at is not None:
                        pool.memset(gat[:, :, :, ones_at:ones_at + 1], 1.0).then_inc(s_zero, 1)

                    def gather(i, r):
                        k = i * RING + r
                        pool.wait_ge(s_rec[r], i * 16 + 16)
                        pool.sem_inc(s_turn, 1)
                        if not isinstance(i, int) or i > 0:
                            pool.wait_ge(s_ag, k - RING + 1)
                            pool.sem_inc(s_turn, 1)
                        for t in range(CH):
                            pool.indirect_dma_start(gat[:, r, t, 0:width], None, table,
                                                    bass.IndirectOffsetOnAxis(ap=rec[:, r, t, DST_AT:DST_AT + 1].bitcast(i32), axis=0)).then_inc(s_gat[r], 16)
                    looped(pool, CHUNKS // RING, lambda i: [gather(i, r) for r in range(RING)])

                @block.vector
                def _(v):
                    v.memset(into_tile, 0.0).then_inc(s_zero, 1)
                    v.wait_ge(s_zero, 2 if ones_at is not None else 1)

                    def one_hot(k, i, r):
                        v.wait_ge(s_rec[r], i * 16 + 16)
                        wait(v, s_ag, k - RING + 1)
                        for t in range(CH):
                            v.tensor_scalar(hot[:, r, t, :], iota_n[:, :], rec[:, r, t, LO_AT:LO_AT + 1], rec[:, r, t, W_AT:W_AT + 1],
                                            ALU.is_equal, ALU.mult).then_inc(s_hot, 1)

                    def add(k, r, blocks):
                        v.wait_ge(s_ag, k + 1)
                        for t in range(CH):
                            into = into_tile[:, bass.ds(blocks[t], 1), :].rearrange("p a f -> p (a f)")
                            wait(v, s_add, k * CH + t)
                            v.tensor_tensor(into, into, bank(r, t), ALU.add).then_inc(s_add, 1)

                    def chunk(i):
                        first = isinstance(i, int)
                        skip = CH if first else 0
                        blocks = [None] * skip + tile_blocks(v, i * (RING * CH) - CH + skip, RING * CH - skip)
                        for r in range(RING):
                            k = i * RING + r
                            one_hot(k, i, r)
                            if not (first and r == 0):
                                add(k - 1, (r - 1) % RING, blocks[r * CH:(r + 1) * CH])
                    looped(v, CHUNKS // RING, chunk)
                    add(CHUNKS - 1, RING - 1, tile_blocks(v, (CHUNKS - 1) * CH, CH))

                @block.tensor
                def _(pe):
                    pe.wait_ge(s_zero, 2 if ones_at is not None else 1)

                    def sums(i, r):
                        k = i * RING + r
                        pe.wait_ge(s_hot, k * CH + CH)
                        pe.wait_ge(s_gat[r], i * (16 * CH) + 16 * CH)
                        wait(pe, s_add, (k - RING + 1) * CH)
                        for t in range(CH):
                            last = pe.matmul(bank(r, t), hot[:, r, t, :], gat[:, r, t, 0:cols], start=True, stop=True)
                        last.then_inc(s_ag, 1)
                    looped(pe, CHUNKS // RING, lambda i: [sums(i, r) for r in range(RING)])

        sums1 = big_a[:, :, 0:2 * FO + 1]
        hop_pass("f", hop_tab, 2 * FO, 2 * FO, sums1)
        with ExitStack() as st:
            s_t2 = sem("t2_stored")
            block = st.enter_context(nc.Block())

            @block.sync
            def _(sp):
                sp.dma_start(hop2_tab.rearrange("(b p) w -> p b w", p=P), big_a[:, :, FO:2 * FO + 1]).then_inc(s_t2, 16)
                sp.wait_ge(s_t2, 16)
        sums2 = big_b[:, :, 0:FO + 1]
        hop_pass("g", hop2_tab, FO + 1, None, sums2)

        with ExitStack() as st:
            BL = 4
            ST = NB // BL
            bh = sb("bh", [P, 2, FO], stack=st)
            fcs = sb("fcs", [P, 2, FO], stack=st)
            bfs = sb("bfs", [P, 2], stack=st)
            xr = sb("xr", [P, 2, BL, 2, FO], stack=st)
            res = sb("res", [P, 2, BL, 2, FO], stack=st)
            y = sb("y", [P, 2, BL, 2, FO], stack=st)
            z = sb("z", [P, BL, 2, FO], stack=st)
            neg = sb("neg", [P, BL, 2, FO], stack=st)
            pos = sb("pos_rows", [P, BL, 2, FO], stack=st)
            mask = sb("mask", [P, 2, NB], stack=st)
            inv = sb("inv", [P, 2, NB], stack=st)
            gate = sb("gate", [P, 2, BL, 2], stack=st)
            s_w, s_g, s_gs = sem("o_weights"), sem("o_gate"), sem("o_sigmoid")
            s_x, s_out = [sem("o_x1_0"), sem("o_x1_1")], [sem("o_stored0"), sem("o_stored1")]
            s_out_turn = sem("o_turn")
            s_inv, s_y, s_z, s_parts, s_res = sem("o_inverse"), sem("o_rows"), sem("o_gate_rows"), sem("o_parts"), sem("o_result")
            x1_v = x1_dr.rearrange("(b p) f -> p b f", p=P)
            out_v = out.rearrange("(b p) f -> p b f", p=P)
            block = st.enter_context(nc.Block())

            @block.sync
            def _(sp):
                sp.dma_start(bh[:, :, :].rearrange("p a b -> p (a b)"), b_hop.partition_broadcast(P)).then_inc(s_w, 16)
                sp.dma_start(fcs[:, :, :].rearrange("p a b -> p (a b)"), fc.partition_broadcast(P)).then_inc(s_w, 16)
                sp.dma_start(bfs[:, :], bf.partition_broadcast(P)).then_inc(s_w, 16)

                def steps(i):
                    for u in range(2):
                        n = i * 2 + u
                        wait(sp, s_res, n - 1)
                        sp.dma_start(xr[:, u, :, :, :].rearrange("p b h f -> p b (h f)"), x1_v[:, bass.ds(n * BL, BL), :]).then_inc(s_x[u], 16)
                looped(sp, ST // 2, steps)

            @block.gpsimd
            def _(pool):
                with pool.Fori(0, ST // 2) as i:
                    for u in range(2):
                        n = i * 2 + u
                        pool.wait_ge(s_res, n + 1)
                        pool.sem_inc(s_out_turn, 1)
                        pool.dma_start(out_v[:, bass.ds(n * BL, BL), :], res[:, u, :, :, :].rearrange("p b h f -> p b (h f)")).then_inc(s_out[u], 16)
                for u in range(2):
                    pool.wait_ge(s_out[u], ST // 2 * 16)

            @block.vector
            def _(v):
                v.wait_ge(s_w, 48)
                done = [0]

                def link(*both):
                    for ins in both:
                        done[0] += 1
                        ins.then_inc(s_inv, 1)
                    v.wait_ge(s_inv, done[0])

                degs = [big_a[:, :, 2 * FO], big_b[:, :, FO]]
                link(*[v.tensor_single_scalar(mask[:, h, :], degs[h], 0.0, op=ALU.is_gt) for h in range(2)])
                link(*[v.tensor_tensor(inv[:, h, :], degs[h], mask[:, h, :], ALU.mult) for h in range(2)])
                link(v.scalar_tensor_tensor(out=inv[:, :, :], in0=inv[:, :, :], scalar=1.0, in1=mask[:, :, :], op0=ALU.add, op1=ALU.subtract))
                link(v.reciprocal(inv[:, :, :], inv[:, :, :]))
                link(v.tensor_tensor(inv[:, :, :], inv[:, :, :], mask[:, :, :], ALU.mult))

                def gates(n, u):
                    for h, big in enumerate((big_a, big_b)):
                        v.tensor_tensor(y[:, u, :, h, :], big[:, bass.ds(n * BL, BL), 0:FO],
                                        inv[:, h, bass.ds(n * BL, BL)].unsqueeze(2).to_broadcast([P, BL, FO]), ALU.mult).then_inc(s_y, 1)
                    v.wait_ge(s_y, n * 3 + 2)
                    v.tensor_tensor(y[:, u, :, :, :], y[:, u, :, :, :], bh[:, :, :].unsqueeze(1).to_broadcast([P, BL, 2, FO]), ALU.add).then_inc(s_y, 1)
                    v.wait_ge(s_y, n * 3 + 3)
                    v.tensor_tensor(z[:, :, :, :], y[:, u, :, :, :], fcs[:, :, :].unsqueeze(1).to_broadcast([P, BL, 2, FO]), ALU.mult).then_inc(s_z, 1)
                    v.wait_ge(s_z, n + 1)
                    v.tensor_reduce(gate[:, u, :, :], z[:, :, :, :], AX.X, ALU.add).then_inc(s_g, 1)

                def rows_of(tile):
                    return tile.rearrange("p b h f -> p (b h) f")

                def rows(n, i, u):
                    v.wait_ge(s_x[u], i * 16 + 16)
                    wait(v, s_res, n)
                    v.scalar_tensor_tensor(out=pos[:, :, :, :], in0=y[:, u, :, :, :], scalar=0.0, in1=xr[:, u, :, :, :],
                                            op0=ALU.max, op1=ALU.add).then_inc(s_parts, 1)
                    v.wait_ge(s_gs, n * 2 + 2)
                    v.scalar_tensor_tensor(out=rows_of(neg[:, :, :, :]), in0=rows_of(y[:, u, :, :, :]), scalar=0.0,
                                           in1=gate[:, u, :, :].rearrange("p b h -> p (b h)").unsqueeze(2).to_broadcast([P, 2 * BL, FO]), op0=ALU.min, op1=ALU.mult).then_inc(s_parts, 1)
                    v.wait_ge(s_parts, n * 2 + 2)
                    wait(v, s_out[u], i * 16)
                    v.tensor_tensor(res[:, u, :, :, :], pos[:, :, :, :], neg[:, :, :, :], ALU.add).then_inc(s_res, 1)

                def steps(i):
                    for u in range(2):
                        n = i * 2 + u
                        gates(n, u)
                        if not (isinstance(n, int) and n == 0):
                            rows(n - 1, i if u else i - 1, 1 - u)
                steps(0)
                steps(1)
                with v.Fori(2, ST // 2) as i:
                    steps(i)
                rows(ST - 1, ST // 2 - 1, 1)

            @block.scalar
            def _(act):
                act.wait_ge(s_w, 48)
                with act.Fori(0, ST // 2) as i:
                    for u in range(2):
                        act.wait_ge(s_g, i * 2 + u + 1)
                        for h in range(2):
                            act.activation(gate[:, u, :, h], gate[:, u, :, h], ACT.Sigmoid, bias=bfs[:, h:h + 1]).then_inc(s_gs, 1)


def kernel(x, src, dst, edge_attr_16, edge_weight, L0_gnn_eW1, L0_gnn_eb1, L0_gnn_eW2, L0_gnn_eb2, L0_gnn_nW1,
           L0_gnn_nb1, L0_gnn_nW2, L0_gnn_nb2, L1_gnn_W0, L1_gnn_b0, L1_gnn_W1, L1_gnn_b1, L1_gnn_fc0, L1_gnn_bf0,
           L1_gnn_fc1, L1_gnn_bf1):
    import numpy as np
    import concourse.bacc as bacc
    from concourse import mybir as mb
    from concourse.bass_utils import run_bass_kernel_spmd as run

    x, src, dst, attr, weight = map(np.asarray, (x, src, dst, edge_attr_16, edge_weight))
    eW1, nW1 = np.asarray(L0_gnn_eW1), np.asarray(L0_gnn_nW1)
    n, e = x.shape[0], src.shape[0]
    blocks, cols = sizes(n, e)
    x_pad = np.zeros((blocks * P, D), np.float32)
    x_pad[:n] = x
    src_pad = np.full(P * cols, blocks * P - 1, np.int32)
    src_pad[:e] = src
    edges = np.zeros((P * cols, IN_WORDS), np.float32)
    edges[:e, :DE] = attr
    edges[:e, W_IN] = weight
    edges.view(np.int32)[:e, DST_IN] = dst
    row = lambda *parts: np.concatenate([np.asarray(p).reshape(-1) for p in parts])
    ins = {
        "x": x_pad, "src": src_pad.reshape(P, cols), "edges": edges,
        "w_node": np.concatenate([eW1[:D], eW1[D:2 * D], nW1[:D]], axis=1),
        "b_node": row(L0_gnn_eb1, np.zeros(D, np.float32), L0_gnn_nb1),
        "w_edge": np.tile(eW1[2 * D:], (P // DE, 1)), "e_w2": np.asarray(L0_gnn_eW2),
        "e_b2": row(L0_gnn_eb2),
        "w_update": np.concatenate([nW1[D:], np.asarray(L0_gnn_nW2), np.asarray(L1_gnn_W0), np.asarray(L1_gnn_W1)], axis=1),
        "n_b2": row(L0_gnn_nb2), "b_hop": row(L1_gnn_b0, L1_gnn_b1), "fc": row(L1_gnn_fc0, L1_gnn_fc1),
        "bf": row(L1_gnn_bf0, L1_gnn_bf1),
    }
    ins = {k: np.ascontiguousarray(v) for k, v in ins.items()}
    nc = bacc.Bacc("TRN2", target_bir_lowering=False, num_devices=1)
    args = [nc.dram_tensor("in_" + k, v.shape, mb.dt.from_np(v.dtype), kind="ExternalInput").ap() for k, v in ins.items()]
    out = nc.dram_tensor("out", (blocks * P, D), mb.dt.float32, kind="ExternalOutput").ap()
    gnn(nc, n, e, *args, out)
    r = run(nc, [{"in_" + k: v for k, v in ins.items()}], core_ids=[0])
    return r.results[0]["out"][:n]
```
